# Optimizing a Trainium2 kernel written in Bass

```python
import numpy as np
import jax
import jax.numpy as jnp

def _softmax(x, axis=-1):
    return jax.nn.softmax(x, axis=axis)

def _gelu(x):
    return jax.nn.gelu(x, approximate=True)

def _silu(x):
    return jax.nn.silu(x)

def _sigmoid(x):
    return jax.nn.sigmoid(x)

def _layernorm(x, axis=-1, eps=1e-05):
    m = jnp.mean(x, axis=axis, keepdims=True)
    v = jnp.var(x, axis=axis, keepdims=True)
    return (x - m) / jnp.sqrt(v + eps)

def _scatter_add(tgt, idx, src, axis=0):
    return tgt.at[idx].add(src)

def _segment_sum(src, seg, n):
    return jax.ops.segment_sum(src, seg, n)
kernel_name = 'mk_adaln_d1_jaxref_r8_53580a'

def setup_inputs(seed: int=0):
    np.random.seed(seed)
    _w = jnp.asarray

    def _L0_attn_setup():
        import math
        import jax, jax.numpy as jnp
        import numpy as np
        B, T, D = (8, 256, 128)

        def _gelu(x):
            c = math.sqrt(2.0 / math.pi)
            return 0.5 * x * (1.0 + jnp.tanh(c * (x + 0.044715 * x * x * x)))

        def _normalize(x, axis):
            n = jnp.linalg.norm(x, axis=axis, keepdims=True)
            return x / jnp.maximum(n, 1e-12)
        key = jax.random.key(seed)
        k1, k2 = jax.random.split(key)
        x = jax.random.normal(k1, (B, T, D), dtype=jnp.float32)
        ema_out = _normalize(jax.random.normal(k2, (D,), dtype=jnp.float32), 0)[..., 0] if False else None
        ema = jax.random.normal(k2, (D,), dtype=jnp.float32)
        ema = ema / jnp.maximum(jnp.linalg.norm(ema), 1e-12)
        return {'x': x, 'ema_out': ema, 'logit_decay': jnp.float32(math.log(0.9 / 0.1)), 'log_tau': jnp.float32(math.log(2.0)), 'log_blend': jnp.float32(math.log(0.3 / 0.7)), 'logit_blend_seq': jnp.float32(0.0)}
    _L0_attn_in = _L0_attn_setup()

    def _L0_ffn_setup():
        import jax, jax.numpy as jnp
        import numpy as np
        D_MODEL = 128
        D_FF = 512
        N_EXPERTS = 8
        INIT_SCALE = 0.1

        def _trunc_normal(key, shape, std):
            return std * jax.random.truncated_normal(key, -2.0, 2.0, shape, dtype=jnp.float32)
        key = jax.random.key(seed)
        ks = jax.random.split(key, 5)
        x = jax.random.normal(ks[0], (4, 128, D_MODEL), dtype=jnp.float32)
        router_W = _trunc_normal(ks[1], (D_MODEL, N_EXPERTS), INIT_SCALE / np.sqrt(D_MODEL))
        router_b = jnp.zeros((N_EXPERTS,), dtype=jnp.float32)
        W1 = _trunc_normal(ks[2], (N_EXPERTS, D_MODEL, D_FF), INIT_SCALE / np.sqrt(D_MODEL))
        b1 = jnp.zeros((N_EXPERTS, D_FF), dtype=jnp.float32)
        W2 = _trunc_normal(ks[3], (N_EXPERTS, D_FF, D_MODEL), INIT_SCALE / np.sqrt(D_FF))
        b2 = jnp.zeros((N_EXPERTS, D_MODEL), dtype=jnp.float32)
        return {'x': x, 'router_W': router_W, 'router_b': router_b, 'W1': W1, 'b1': b1, 'W2': W2, 'b2': b2}
    _L0_ffn_in = _L0_ffn_setup()
    _L0_c = _w((lambda *s: np.random.randn(*s).astype(np.float32) * 0.05)(4, 128))
    _L0_wmod = _w((lambda *s: np.random.randn(*s).astype(np.float32) * 0.05)(128, 6 * 128) * 128 ** (-0.5))
    _d = {'L0_attn_x': _L0_attn_in['x'], 'L0_attn_ema_out': _L0_attn_in['ema_out'], 'L0_attn_logit_decay': _L0_attn_in['logit_decay'], 'L0_attn_log_tau': _L0_attn_in['log_tau'], 'L0_attn_log_blend': _L0_attn_in['log_blend'], 'L0_attn_logit_blend_seq': _L0_attn_in['logit_blend_seq'], 'L0_ffn_router_W': _L0_ffn_in['router_W'], 'L0_ffn_router_b': _L0_ffn_in['router_b'], 'L0_ffn_W1': _L0_ffn_in['W1'], 'L0_ffn_b1': _L0_ffn_in['b1'], 'L0_ffn_W2': _L0_ffn_in['W2'], 'L0_ffn_b2': _L0_ffn_in['b2'], 'L0_c': _L0_c, 'L0_wmod': _L0_wmod}
    _x0 = _d['L0_attn_x']
    _d['L0_attn_x'] = jax.random.normal(jax.random.fold_in(jax.random.key(seed), 1), (4, 1024, 128), dtype=_x0.dtype)
    del _x0
    return _d

def reference(L0_attn_x, L0_attn_ema_out, L0_attn_logit_decay, L0_attn_log_tau, L0_attn_log_blend, L0_attn_logit_blend_seq, L0_ffn_router_W, L0_ffn_router_b, L0_ffn_W1, L0_ffn_b1, L0_ffn_W2, L0_ffn_b2, L0_c, L0_wmod):

    def _L0_attn_ref(x, ema_out, logit_decay, log_tau, log_blend, logit_blend_seq):
        import math
        import jax, jax.numpy as jnp
        import numpy as np
        B, T, D = (8, 256, 128)

        def _gelu(x):
            c = math.sqrt(2.0 / math.pi)
            return 0.5 * x * (1.0 + jnp.tanh(c * (x + 0.044715 * x * x * x)))

        def _normalize(x, axis):
            n = jnp.linalg.norm(x, axis=axis, keepdims=True)
            return x / jnp.maximum(n, 1e-12)
        Bx, Tx, Dx = x.shape
        tau = jnp.exp(log_tau)
        alpha = jax.nn.sigmoid(log_blend)
        w_seq = jax.nn.sigmoid(logit_blend_seq)
        out = _gelu(x)
        out_norm = _normalize(out, -1)
        ema_norm = ema_out / jnp.maximum(jnp.linalg.norm(ema_out), 1e-12)
        ema_sim = jnp.einsum('btd,d->bt', out_norm, ema_norm)
        sim_mat = jnp.einsum('btd,bsd->bts', out_norm, out_norm)
        causal = jnp.tril(jnp.ones((Tx, Tx), dtype=bool), k=-1)
        sim_past = jnp.where(causal[None], sim_mat, -2.0)
        seq_sim = jnp.max(sim_past, axis=-1)
        has_past = (jnp.arange(Tx) > 0)[None, :]
        seq_sim = jnp.where(has_past, seq_sim, ema_sim)
        familiarity = w_seq * seq_sim + (1.0 - w_seq) * ema_sim
        novelty = jnp.exp(-tau * familiarity)
        gate = 1.0 - alpha + alpha * novelty
        return out * gate[..., None]

    def _L0_ffn_ref(x, router_W, router_b, W1, b1, W2, b2):
        import jax, jax.numpy as jnp
        import numpy as np
        D_MODEL = 128
        D_FF = 512
        N_EXPERTS = 8
        INIT_SCALE = 0.1

        def _trunc_normal(key, shape, std):
            return std * jax.random.truncated_normal(key, -2.0, 2.0, shape, dtype=jnp.float32)
        logits = jnp.einsum('bsd,de->bse', x.astype(jnp.float32), router_W) + router_b
        probs = jax.nn.softmax(logits, axis=-1)
        top1 = jnp.argmax(probs, axis=-1)
        mask = jax.nn.one_hot(top1, N_EXPERTS, dtype=x.dtype)
        gates = mask * probs.astype(x.dtype)
        h = jax.nn.relu(jnp.einsum('bsd,edf->besf', x, W1) + b1[:, None, :])
        y = jnp.einsum('besf,efd->besd', h, W2) + b2[:, None, :]
        out = jnp.einsum('bse,besd->bsd', gates, y)
        return out
    x = L0_attn_x
    mod = (_silu(L0_c) @ L0_wmod).reshape(L0_c.shape[0], 6, 1, -1)
    sa, ca, ga, sb, cb, gb = (mod[:, 0], mod[:, 1], mod[:, 2], mod[:, 3], mod[:, 4], mod[:, 5])
    ga = (2 * (ga >= 0) - 1) * jnp.maximum(jnp.abs(ga), 0.25)
    gb = (2 * (gb >= 0) - 1) * jnp.maximum(jnp.abs(gb), 0.25)
    h = _layernorm(x, axis=-1) * (1 + ca) + sa
    x = x + ga * _L0_attn_ref(h, L0_attn_ema_out, L0_attn_logit_decay, L0_attn_log_tau, L0_attn_log_blend, L0_attn_logit_blend_seq)
    h = _layernorm(x, axis=-1) * (1 + cb) + sb
    x = x + gb * _L0_ffn_ref(h, L0_ffn_router_W, L0_ffn_router_b, L0_ffn_W1, L0_ffn_b1, L0_ffn_W2, L0_ffn_b2)
    return x

_drawn_inputs = setup_inputs


def setup_inputs(seed=0):
    import zlib

    import numpy as np

    out = dict(_drawn_inputs(seed))
    spreads = {'L0_ffn_router_b': (0.0, 0.8), 'L0_ffn_b1': (0.0, 0.8), 'L0_ffn_b2': (0.0, 0.8)}
    factors = {'L0_attn_ema_out': 8.0, 'L0_ffn_router_W': 8.0, 'L0_ffn_W1': 8.0, 'L0_ffn_W2': 8.0}
    for name, (base, spread) in spreads.items():
        noise = np.random.default_rng([zlib.crc32(name.encode()), seed]).standard_normal(out[name].shape)
        drawn = base * np.exp(spread * noise) if base else spread * noise
        out[name] = jnp.asarray(drawn.astype(out[name].dtype))
    for name, factor in factors.items():
        out[name] = (out[name] * factor).astype(out[name].dtype)
    return out
```

```python
import concourse.bass as bass
from concourse import mybir
from contextlib import ExitStack

f32, bf16, i32 = mybir.dt.float32, mybir.dt.bfloat16, mybir.dt.int32
ALU = mybir.AluOpType
ACT = mybir.ActivationFunctionType
AX = mybir.AxisListType

B, T, D = 4, 1024, 128
P = 128
NT = T // P
E, F = 8, 512
FC = F // P
TOKENS = B * T
TILES = (TOKENS + E * (P - 1)) // P
REGION = TOKENS + P
DUMMY = TILES - TOKENS // P
H2, X1, GG, TOK = 0, D, 2 * D, 3 * D
ROW = 3 * D + 4
LN_EPS = 1e-5
GELU_A = 0.044715
GELU_C = 0.7978845608028654
MASKED = -4.0
SLOTS = 6
SA, CA, GA, SB, CB, GB = range(6)


def wait_for(eng, sem, value):
    if not (isinstance(value, int) and value <= 0):
        eng.wait_ge(sem, value)


def build(nc, x_d, ema_d, decay_d, tau_d, blend_d, seq_d, rw_d, rb_d, w1_d, b1_d, w2_d, b2_d, c_d, wmod_d, out_d):
    ctx = ExitStack()
    with ctx:
        def sb(name, shape, dt=f32):
            return ctx.enter_context(nc.sbuf_tensor(name, shape, dt))

        def sem(name):
            return ctx.enter_context(nc.semaphore(name))

        rows_d = nc.dram_tensor("expert_rows", [E * REGION + DUMMY * P, ROW], f32, kind="Internal").ap()
        out_rows = out_d.rearrange("b t d -> (b t) d")

        ident = sb("ident", [P, P])
        ident_h = sb("ident_h", [P, P], bf16)
        mask_h = sb("mask_h", [P, P], bf16)
        before_h = sb("before_h", [P, P], bf16)
        ones_h = sb("ones_h", [P, P], bf16)
        ones = sb("ones", [P, P])
        minus_half = sb("minus_half", [P, NT])
        exp_less8 = sb("exp_less8", [P, NT, E])
        exp_base = sb("exp_base", [P, NT, E])
        row128 = sb("row128", [1, E, TOKENS // P])
        upto = sb("upto", [1, E, E])
        tile_no = sb("tile_no", [1, TILES, E])
        tok_no = sb("tok_no", [P, B * NT], i32)
        pad_row = sb("pad_row", [P, ROW])
        w1 = sb("w1", [P, E * F])
        w2 = sb("w2", [P, E * FC * D])
        b1 = sb("b1", [P, E * F])
        b2 = sb("b2", [P, E * D])
        rw = sb("rw", [P, E])
        rb = sb("rb", [P, E])
        wmod = sb("wmod", [P, 6 * D])
        mods = sb("mods", [P, B, 6, D])
        c4 = sb("c4", [B, D])
        sil = sb("sil", [P, 4, B])
        sil_b = sb("sil_b", [P, B, P])
        ema = sb("ema", [P, 4])
        scal = sb("scal", [P, 3])
        scal2 = sb("scal2", [P, 8])
        gsign = sb("gsign", [P, 2, D])
        gabs = sb("gabs", [P, 2, D])
        gmag = sb("gmag", [P, 2, D])

        xa = sb("xa", [P, NT, D])
        xr = sb("xr", [P, NT, D])
        st1 = sb("st1", [P, NT, 6])
        mv1 = sb("mv1", [P, NT, 2])
        var1 = sb("var1", [P, NT])
        rstd1 = sb("rstd1", [P, NT])
        nbias1 = sb("nbias1", [P, NT])
        xn1 = sb("xn1", [P, NT, D])
        hm1 = sb("hm1", [P, NT, D])
        h1 = sb("h1", [P, NT, D])
        sq = sb("sq", [P, NT, D])
        wg = sb("wg", [P, NT, D])
        th = sb("th", [P, NT, D])
        out2 = sb("out2", [P, NT, D])
        og = sb("og", [P, NT, D])
        junk = sb("junk", [P, NT, D])
        ss = sb("ss", [P, NT])
        ssc = sb("ssc", [P, NT])
        rn = sb("rn", [P, NT])
        on = sb("on", [P, NT, D])
        onT = sb("onT", [P, T])
        mx = sb("mx", [P, NT])
        fam1 = sb("fam1", [P, NT])
        fam = sb("fam", [P, NT])
        nov = sb("nov", [P, NT])
        gate = sb("gate", [P, NT])
        rows2 = [sb(f"rows{i}", [P, NT, ROW]) for i in range(2)]
        st2 = sb("st2", [P, NT, 6])
        mv2 = sb("mv2", [P, NT, 2])
        var2 = sb("var2", [P, NT])
        rstd2 = sb("rstd2", [P, NT])
        nbias2 = sb("nbias2", [P, NT])
        xn2 = sb("xn2", [P, NT, D])
        hm2 = sb("hm2", [P, NT, D])
        h2T = sb("h2T", [P, T])
        lg = sb("lg", [P, NT, E])
        lmax = sb("lmax", [P, NT])
        lz = sb("lz", [P, NT, E])
        lexp = sb("lexp", [P, NT, E])
        lsum = sb("lsum", [P, NT])
        top = sb("top", [P, NT])
        cand = sb("cand", [P, NT, E])
        cmin = sb("cmin", [P, NT])
        hot = sb("hot", [P, NT, E], bf16)
        hot_new = sb("hot_new", [P, E])
        hot_sum = sb("hot_sum", [P, E], bf16)
        placed = sb("placed", [P, NT, E])
        placed2 = sb("placed2", [P, NT, E])
        posf = sb("posf", [P, NT])
        pos2 = [sb(f"pos{i}", [P, NT], i32) for i in range(2)]

        cnt = sb("cnt", [1, E])
        cmp1 = sb("cmp1", [1, E, TOKENS // P])
        ntile = sb("ntile", [1, E])
        cum = sb("cum", [1, E, E])
        tend = sb("tend", [1, E])
        past = sb("past", [1, TILES, E])
        past_n = sb("past_n", [1, TILES, E])
        ek = sb("ek", [1, TILES])
        skipped = sb("skipped", [1, TILES])
        rk = sb("rk", [1, TILES])
        rk2 = sb("rk2", [1, TILES])
        tile_exp = sb("tile_exp", [1, TILES], i32)
        tile_row = sb("tile_row", [1, TILES], i32)
        pad_at = sb("pad_at", [1, E], i32)

        tb = [sb(f"tb{s}", [P, ROW]) for s in range(SLOTS)]
        ob = [sb(f"ob{s}", [P, D]) for s in range(SLOTS)]
        tok = [sb(f"tok{s}", [P, 1], i32) for s in range(SLOTS)]
        h2s = [sb(f"h2s{s}", [P, P]) for s in range(2)]
        hid = [sb(f"hid{s}", [P, F]) for s in range(2)]
        hidT = [sb(f"hidT{s}", [P, F]) for s in range(2)]
        y1 = sb("y1", [P, D])
        y2 = sb("y2", [P, D])

        banks = ctx.enter_context(nc.psum_tensor("banks", [P, 8, 512], f32))
        p_turn = banks[:, 0:2, :].rearrange("p a n -> p (a n)")
        p_sim = [banks[:, 2:4, :].rearrange("p a n -> p (a n)"), banks[:, 4:6, :].rearrange("p a n -> p (a n)")]
        p_ema = banks[:, 6, 0:NT]
        p_logit = banks[:, 7, 0:NT * E].rearrange("p (t e) -> p t e", e=E)
        p_rank = banks[:, 7, NT * E:2 * NT * E].rearrange("p (t e) -> p t e", e=E)
        p_count = banks[:, 7, 0:E]
        p_h2T = [banks[:, a, 0:P] for a in (0, 1)]
        p_hid = [banks[:, a, :] for a in (2, 3)]
        p_hidT = [banks[:, a, :] for a in (4, 5)]
        p_y = [banks[:, a, 0:D] for a in (6, 7)]

        names = """ld_xa ld_xr ld_c ld_wmod ld_small ld_ema ld_w1 ld_w2 ld_b dummy_out pads_out
            pool_own consts ema_sq ema_ss ema_cl ema_rn ema_n c_T c_exp c_sil mod_ps mod_sb mods_ok scal_e scal_ok dve_prep
            bn1 mv1_d var1_d pw1 nb1 xn1_d hm1_d h1_d sq_d wg_d th_d out2_d og_d ss_d ssc_d pwn on_d
            tr1 onT_d ema_d2 sim_d mx_d fam1_d fam_d nov_d gate_d x1_d bn2 mv2_d var2_d pw2 nb2 xn2_d hm2_d h2_d
            tr2 h2T_d rt_d lg_d lmax_d lz_d lexp_d lsum_d top_d cand_d cmin_d hot_d rank_d hotn_d hots_d pl_d pl2_d posf_d pos_d
            gg_d tok_d cnt_d tab_own table_d
            t_h2T t_h2s t_hid t_hidb t_hidT t_hidr t_y t_y1 t_y2 t_fin put_turn""".split()
        S = {n: sem(n) for n in names}
        rows_out = [sem(f"rows_out{i}") for i in range(2)]
        loaded = [sem(f"loaded{s}") for s in range(SLOTS)]
        stored = [sem(f"stored{s}") for s in range(SLOTS)]

        block = ctx.enter_context(nc.Block())

        def mod(b, which):
            return mods[:, b, which:which + 1, :].to_broadcast([P, NT, D])

        def per_tile(col):
            return col.unsqueeze(2).to_broadcast([P, NT, D])

        def per_exp(col):
            return col.unsqueeze(2).to_broadcast([P, NT, E])

        def tile_at(i, j, d):
            q = 3 + j - d
            return 6 * i + q, q % SLOTS, i + q // SLOTS

        def steps(eng, step):
            for j in range(3, SLOTS):
                step(-1, j)
            for j in range(SLOTS):
                step(0, j)
            with eng.Fori(1, (TILES - 3) // SLOTS) as i:
                for j in range(SLOTS):
                    step(i, j)
            for j in range(3):
                step((TILES - 3) // SLOTS, j)

        def lives(i, j, d):
            n = tile_at(i, j, d)[0]
            return not isinstance(n, int) or 0 <= n < TILES

        @block.sync
        def _(sp):
            sp.dma_start(c4[:, :], c_d).then_inc(S["ld_c"], 16)
            sp.dma_start(xa[:, :, :], x_d[0].rearrange("(t p) d -> p t d", p=P)).then_inc(S["ld_xa"], 16)
            sp.dma_start(wmod[:, :], wmod_d).then_inc(S["ld_wmod"], 16)
            sp.dma_start(xr[:, :, :], x_d[0].rearrange("(t p) d -> p t d", p=P)).then_inc(S["ld_xr"], 16)
            sp.wait_ge(S["consts"], 1)
            sp.dma_start(rows_d[E * REGION:E * REGION + DUMMY * P, :].rearrange("(j p) c -> p j c", p=P),
                         pad_row[:, :].unsqueeze(1).to_broadcast([P, DUMMY, ROW])).then_inc(S["dummy_out"], 16)

            def step(b):
                src = x_d[b + 1].rearrange("(t p) d -> p t d", p=P)
                sp.wait_ge(S["xn1_d"], 8 * b + 8)
                sp.dma_start(xa[:, :, :], src).then_inc(S["ld_xa"], 16)
                if b >= 1:
                    load_xr(b)

            def load_xr(b):
                sp.wait_ge(S["x1_d"], 8 * b)
                sp.dma_start(xr[:, :, :], x_d[b].rearrange("(t p) d -> p t d", p=P)).then_inc(S["ld_xr"], 16)
            for b in range(B - 1):
                step(b)
            load_xr(B - 1)

            sp.wait_ge(S["table_d"], 1)
            for e in range(E):
                at = sp.value_load(pad_at[0:1, e:e + 1], min_val=0, max_val=E * REGION - P)
                sp.dma_start(rows_d[bass.ds(at, P), :], pad_row[:, :]).then_inc(S["pads_out"], 16)
            for q in rows_out:
                sp.wait_ge(q, 16 * NT * B // 2)
            sp.wait_ge(S["pads_out"], 16 * E)
            sp.wait_ge(S["dummy_out"], 16)

            def rnd_is_late(rnd):
                return not (isinstance(rnd, int) and rnd == 0)

            def load(n, slot, rnd):
                wait_for(sp, S["t_fin"], n - SLOTS + 1 if rnd_is_late(rnd) else 0)
                at = sp.value_load(tile_row[0:1, n:n + 1] if isinstance(n, int) else tile_row[0:1, bass.ds(n, 1)],
                                   min_val=0, max_val=E * REGION + (DUMMY - 1) * P)
                sp.dma_start(tb[slot][:, :], rows_d[bass.ds(at, P), :]).then_inc(loaded[slot], 16)

            for slot in range(SLOTS):
                load(slot, slot, 0)
            with sp.Fori(1, TILES // SLOTS) as i:
                for slot in range(SLOTS):
                    load(i * SLOTS + slot, slot, i)
            for n in range(TILES // SLOTS * SLOTS, TILES):
                load(n, n % SLOTS, n // SLOTS)
            for slot in range(SLOTS):
                sp.wait_ge(stored[slot], 16 * ((TILES - 1 - slot) // SLOTS + 1))

        @block.gpsimd
        def _(pool):
            own = [0]

            def chain(ins):
                own[0] += 1
                ins.then_inc(S["pool_own"], 1)
                pool.wait_ge(S["pool_own"], own[0])

            chain(pool.memset(pad_row[:, :], 0.0))
            pool.memset(pad_row[:, TOK:TOK + 1].bitcast(i32), 1 << 20).then_inc(S["consts"], 1)
            pool.memset(minus_half[:, :], -0.5)
            chain(pool.memset(ones[:, :], 1.0))
            chain(pool.memset(ident[:, :], 0.0))
            pool.affine_select(out=ident[:, :], in_=ident[:, :], compare_op=ALU.not_equal, fill=1.0, base=0,
                               pattern=[[-1, P]], channel_multiplier=1).then_inc(S["consts"], 1)
            chain(pool.memset(ident_h[:, :], 0.0))
            chain(pool.memset(mask_h[:, :], 0.0))
            chain(pool.memset(before_h[:, :], 1.0))
            chain(pool.memset(ones_h[:, :], 1.0))
            pool.affine_select(out=ident_h[:, :], in_=ident_h[:, :], compare_op=ALU.not_equal, fill=1.0, base=0,
                               pattern=[[-1, P]], channel_multiplier=1).then_inc(S["consts"], 1)
            pool.affine_select(out=mask_h[:, :], in_=mask_h[:, :], compare_op=ALU.is_gt, fill=MASKED, base=0,
                               pattern=[[-1, P]], channel_multiplier=1).then_inc(S["consts"], 1)
            pool.affine_select(out=before_h[:, :], in_=before_h[:, :], compare_op=ALU.is_gt, fill=0.0, base=0,
                               pattern=[[1, P]], channel_multiplier=-1).then_inc(S["consts"], 1)
            chain(pool.memset(hot_sum[:, :], 0.0))
            for rows in rows2:
                chain(pool.memset(rows[:, :, TOK + 1:ROW], 0.0))

            def pow_half(out, in_, done):
                pool.tensor_tensor(out, in_, minus_half[:, 0:in_.shape[1]], ALU.pow).then_inc(done, 1)

            pool.wait_ge(S["var1_d"], 1)
            pow_half(rstd1[:, :], var1[:, :], S["pw1"])
            pool.wait_ge(S["ema_cl"], 1)
            pow_half(ema[:, 3:4], ema[:, 2:3], S["ema_rn"])
            big = dict(channel_multiplier=0, base=0, allow_small_or_imprecise_dtypes=True)
            pool.iota(exp_less8[:, :, :], [[0, NT], [1, E]], **{**big, "base": -E}).then_inc(S["consts"], 1)
            pool.iota(exp_base[:, :, :], [[0, NT], [REGION, E]], **big).then_inc(S["consts"], 1)
            pool.iota(row128[:, :, :], [[0, E], [P, TOKENS // P]], **big).then_inc(S["consts"], 1)
            pool.iota(tile_no[:, :, :], [[1, TILES], [0, E]], **big).then_inc(S["consts"], 1)
            pool.iota(tok_no[:, :], [[P, B * NT]], base=0, channel_multiplier=1).then_inc(S["consts"], 1)
            chain(pool.memset(upto[:, :, :], 1.0))
            pool.affine_select(out=upto[:, :, :], in_=upto[:, :, :], compare_op=ALU.is_ge, fill=0.0, base=0,
                               pattern=[[1, E], [-1, E]], channel_multiplier=0).then_inc(S["consts"], 1)

            def shift1(b):
                pool.wait_ge(S["hm1_d"], b + 1)
                if b >= 1:
                    pool.wait_ge(S["out2_d"], b)
                pool.tensor_tensor(h1[:, :, :], hm1[:, :, :], mod(b, SA), ALU.add).then_inc(S["h1_d"], 1)

            def scatter(b):
                pool.wait_ge(S["tok_d"], b + 1)
                pool.wait_ge(S["gg_d"], NT * b + NT)
                pool.wait_ge(S["h2_d"], b + 1)
                pool.wait_ge(S["pos_d"], b + 1)
                for t in range(NT):
                    pool.indirect_dma_start(rows_d[:, :], bass.IndirectOffsetOnAxis(ap=pos2[b % 2][:, t:t + 1], axis=0),
                                            rows2[b % 2][:, t, :], None).then_inc(rows_out[b % 2], 16)

            def norm_pow(b):
                pool.wait_ge(S["ssc_d"], b + 1)
                wait_for(pool, S["on_d"], b)
                pow_half(rn[:, :], ssc[:, :], S["pwn"])

            def gated(b):
                pool.wait_ge(S["out2_d"], b + 1)
                wait_for(pool, S["x1_d"], 8 * b)
                pool.tensor_tensor(og[:, :, :], out2[:, :, :], mod(b, GA), ALU.mult).then_inc(S["og_d"], 1)

            def rstd1_of(b):
                pool.wait_ge(S["var1_d"], b + 1)
                wait_for(pool, S["xn1_d"], 8 * b)
                pow_half(rstd1[:, :], var1[:, :], S["pw1"])

            shift1(0)
            norm_pow(0)
            gated(0)
            rstd1_of(1)
            shift1(1)
            for b in range(B):
                if b + 1 < B:
                    norm_pow(b + 1)
                if b >= 1:
                    scatter(b - 1)
                pool.wait_ge(S["var2_d"], b + 1)
                wait_for(pool, S["xn2_d"], 8 * b)
                pow_half(rstd2[:, :], var2[:, :], S["pw2"])
                if b + 2 < B:
                    rstd1_of(b + 2)
                if b + 1 < B:
                    gated(b + 1)
                pool.wait_ge(S["hm2_d"], b + 1)
                pool.tensor_tensor(rows2[b % 2][:, :, H2:H2 + D], hm2[:, :, :], mod(b, SB), ALU.add).then_inc(S["h2_d"], 1)
                if b + 2 < B:
                    shift1(b + 2)
            scatter(B - 1)

            last_row = pool.snap(TOKENS - 1)

            def put(i, j):
                if not lives(i, j, 3):
                    return
                n, slot, rnd = tile_at(i, j, 3)
                pool.wait_ge(S["t_fin"], n + 1)
                pool.sem_inc(S["put_turn"], 1)
                pool.indirect_dma_start(out_rows, bass.IndirectOffsetOnAxis(ap=tok[slot][:, :], axis=0),
                                        ob[slot][:, :], None, bounds_check=last_row, oob_is_err=False)\
                    .then_inc(stored[slot], 16)
            steps(pool, put)

        @block.scalar
        def _(act):
            act.dma_start(scal[:, 0:1], tau_d.unsqueeze(0).to_broadcast([P, 1])).then_inc(S["ld_small"], 16)
            act.dma_start(scal[:, 1:2], blend_d.unsqueeze(0).to_broadcast([P, 1])).then_inc(S["ld_small"], 16)
            act.dma_start(scal[:, 2:3], seq_d.unsqueeze(0).to_broadcast([P, 1])).then_inc(S["ld_small"], 16)
            act.dma_start(ema[:, 0:1], ema_d.unsqueeze(1)).then_inc(S["ld_ema"], 16)
            act.dma_start(rw[:, :], rw_d).then_inc(S["ld_small"], 16)
            act.dma_start(rb[:, :], rb_d.unsqueeze(0).to_broadcast([P, E])).then_inc(S["ld_small"], 16)
            act.wait_ge(S["c_T"], 1)
            act.activation(sil[:, 0, :], banks[:, 7, 0:B], ACT.Exp, scale=-1.0).then_inc(S["c_exp"], 1)
            act.wait_ge(S["ld_small"], 80)
            act.activation(scal2[:, 0:1], scal[:, 0:1], ACT.Exp).then_inc(S["scal_e"], 1)
            act.activation(scal2[:, 1:3], scal[:, 1:3], ACT.Exp, scale=-1.0).then_inc(S["scal_e"], 1)

            def normed(b, src, out, rstd, nbias, ready, done, used):
                act.wait_ge(ready, b + 1)
                if b >= 1:
                    act.wait_ge(used, b)
                for t in range(NT):
                    act.activation(out[:, t, :], src(t), ACT.Identity, bias=nbias[:, t:t + 1],
                                   scale=rstd[:, t:t + 1]).then_inc(done, 1)

            def normed1(b):
                normed(b, lambda t: xa[:, t, :], xn1, rstd1, nbias1, S["nb1"], S["xn1_d"], S["hm1_d"])

            def mods_out(b):
                act.wait_ge(S["mod_ps"], b + 1)
                act.activation(mods[:, b, :, :].rearrange("p a d -> p (a d)"), p_sim[b % 2][:, 0:6 * D], ACT.Copy)\
                   .then_inc(S["mod_sb"], 1)

            mods_out(0)
            normed1(0)
            for b in range(1, B):
                mods_out(b)
            act.dma_start(w1[:, :].rearrange("p (e f) -> p e f", e=E), w1_d.rearrange("e d f -> d e f")).then_inc(S["ld_w1"], 16)
            act.dma_start(w2[:, :].rearrange("p (e c d) -> p e c d", e=E, c=FC),
                          w2_d.rearrange("e (c p) d -> p e c d", p=P)).then_inc(S["ld_w2"], 16)
            act.dma_start(b1[:, :], b1_d.rearrange("e f -> (e f)").unsqueeze(0).to_broadcast([P, E * F])).then_inc(S["ld_b"], 16)
            act.dma_start(b2[:, :], b2_d.rearrange("e d -> (e d)").unsqueeze(0).to_broadcast([P, E * D])).then_inc(S["ld_b"], 16)

            def router_exp(b):
                act.wait_ge(S["lz_d"], b + 1)
                act.activation(lexp[:, :, :], lz[:, :, :], ACT.Exp).then_inc(S["lexp_d"], 1)

            def row_gates(b):
                act.wait_ge(S["top_d"], b + 1)
                src = mods[:, b, GB, :]
                rows = rows2[b % 2]
                wait_for(act, rows_out[b % 2], 16 * NT * (b // 2))
                for t in range(NT):
                    act.activation(rows[:, t, GG:GG + D], src, ACT.Copy, scale=top[:, t:t + 1]).then_inc(S["gg_d"], 1)
                toks = tok_no[:, b * NT:b * NT + NT]
                act.activation(rows[:, :, TOK:TOK + 1].bitcast(i32).squeeze(2), toks, ACT.Copy).then_inc(S["tok_d"], 1)

            def gelu(b):
                act.wait_ge(S["h1_d"], b + 1)
                wait_for(act, S["wg_d"], b)
                act.activation(sq[:, :, :], h1[:, :, :], ACT.Square).then_inc(S["sq_d"], 1)
                act.wait_ge(S["wg_d"], b + 1)
                wait_for(act, S["out2_d"], b)
                act.activation(th[:, :, :], wg[:, :, :], ACT.Tanh, scale=GELU_C * GELU_A).then_inc(S["th_d"], 1)
                act.wait_ge(S["out2_d"], b + 1)
                wait_for(act, S["ssc_d"], b)
                wait_for(act, S["ss_d"], 8 * b)
                for t in range(NT):
                    act.activation(junk[:, t, :], out2[:, t, :], ACT.Square, accum_out=ss[:, t:t + 1]).then_inc(S["ss_d"], 1)

            def turned_out(b, turned, used, dst, done):
                for a in range(2):
                    act.wait_ge(turned, 2 * b + a + 1)
                    if a == 0:
                        wait_for(act, *used)
                    act.activation(dst[:, 512 * a:512 * a + 512], p_turn[:, 512 * a:512 * a + 512], ACT.Copy)\
                       .then_inc(done, 1)

            def onT_out(b):
                turned_out(b, S["tr1"], (S["ema_d2"], b), onT, S["onT_d"])

            def h2T_out(b):
                turned_out(b, S["tr2"], (S["rt_d"], b), h2T, S["h2T_d"])

            gelu(0)
            onT_out(0)
            normed1(1)
            act.wait_ge(S["scal_ok"], 1)
            for b in range(B):
                if b >= 1:
                    h2T_out(b - 1)
                if b + 1 < B:
                    gelu(b + 1)
                if b >= 1:
                    router_exp(b - 1)
                    row_gates(b - 1)
                act.wait_ge(S["fam_d"], b + 1)
                act.activation(nov[:, :], fam[:, :], ACT.Exp, scale=scal2[:, 4:5]).then_inc(S["nov_d"], 1)
                if b + 1 < B:
                    onT_out(b + 1)
                normed(b, lambda t: rows2[b % 2][:, t, X1:X1 + D], xn2, rstd2, nbias2, S["nb2"], S["xn2_d"], S["hm2_d"])
                if b + 2 < B:
                    normed1(b + 2)
            h2T_out(B - 1)
            router_exp(B - 1)
            row_gates(B - 1)

            def tile_step(i, j):
                if lives(i, j, 0):
                    n, slot, _ = tile_at(i, j, 0)
                    act.wait_ge(S["t_h2T"], n + 1)
                    wait_for(act, S["t_hid"], n - 1)
                    act.activation(h2s[slot % 2][:, :], p_h2T[slot % 2], ACT.Copy).then_inc(S["t_h2s"], 1)
                if lives(i, j, 2):
                    n, slot, _ = tile_at(i, j, 2)
                    act.wait_ge(S["t_hidT"], n + 1)
                    act.activation(hidT[slot % 2][:, :], p_hidT[slot % 2], ACT.Relu).then_inc(S["t_hidr"], 1)
            steps(act, tile_step)

        @block.vector
        def _(dve):
            prep = [0]

            def chain(ins):
                prep[0] += 1
                ins.then_inc(S["dve_prep"], 1)
                dve.wait_ge(S["dve_prep"], prep[0])

            def stats(src, st, mv, var, done_bn, done_mv, done_var, b, used):
                for t in range(NT):
                    dve.bn_stats(st[:, t, :], src(t)).then_inc(done_bn, 1)
                dve.wait_ge(done_bn, 8 * b + 8)
                if b >= 1:
                    dve.wait_ge(used, b)
                for t in range(NT):
                    dve.bn_aggr(mv[:, t, :], st[:, t, :]).then_inc(done_mv, 1)
                dve.wait_ge(done_mv, 8 * b + 8)
                dve.tensor_scalar(var[:, :], mv[:, :, 1], LN_EPS, None, ALU.add).then_inc(done_var, 1)

            def norm1(b):
                dve.wait_ge(S["ld_xa"], 16 * b + 16)
                stats(lambda t: xa[:, t, :], st1, mv1, var1, S["bn1"], S["mv1_d"], S["var1_d"], b, S["nb1"])
                dve.wait_ge(S["pw1"], b + 1)
                dve.scalar_tensor_tensor(nbias1[:, :], mv1[:, :, 0], -1.0, rstd1[:, :], ALU.mult, ALU.mult).then_inc(S["nb1"], 1)

            def scale1(b):
                dve.wait_ge(S["xn1_d"], 8 * b + 8)
                if b >= 1:
                    dve.wait_ge(S["h1_d"], b)
                dve.tensor_tensor(hm1[:, :, :], xn1[:, :, :], mod(b, CA), ALU.mult).then_inc(S["hm1_d"], 1)

            def mods_fix(b):
                dve.wait_ge(S["mod_sb"], b + 1)
                c = mods[:, b, CA::3, :]
                g = mods[:, b, GA::3, :]
                dve.tensor_scalar(c, c, 1.0, None, ALU.add).then_inc(S["mods_ok"], 1)
                dve.tensor_scalar(gsign[:, :, :], g, 0.0, 2.0, ALU.is_ge, ALU.mult).then_inc(S["mods_ok"], 1)
                dve.scalar_tensor_tensor(gabs[:, :, :], g, -1.0, g, ALU.mult, ALU.max).then_inc(S["mods_ok"], 1)
                dve.wait_ge(S["mods_ok"], 6 * b + 3)
                dve.tensor_scalar(gmag[:, 0, :], gabs[:, 0, :], 0.25, 0.5, ALU.max, ALU.mult).then_inc(S["mods_ok"], 1)
                dve.tensor_scalar(gmag[:, 1, :], gabs[:, 1, :], 0.25, None, ALU.max).then_inc(S["mods_ok"], 1)
                dve.wait_ge(S["mods_ok"], 6 * b + 5)
                dve.scalar_tensor_tensor(g, gsign[:, :, :], -1.0, gmag[:, :, :], ALU.add, ALU.mult).then_inc(S["mods_ok"], 1)
                dve.wait_ge(S["mods_ok"], 6 * b + 6)

            dve.wait_ge(S["c_exp"], 1)
            chain(dve.tensor_scalar(sil[:, 1, :], sil[:, 0, :], 1.0, None, ALU.add))
            chain(dve.reciprocal(sil[:, 2, :], sil[:, 1, :]))
            chain(dve.tensor_tensor(sil[:, 3, :], sil[:, 2, :], banks[:, 7, 0:B], ALU.mult))
            dve.tensor_copy(sil_b[:, :, :], sil[:, 3, :].unsqueeze(2).to_broadcast([P, B, P])).then_inc(S["c_sil"], 1)
            norm1(0)
            dve.wait_ge(S["ld_ema"], 16)
            dve.tensor_tensor(ema[:, 1:2], ema[:, 0:1], ema[:, 0:1], ALU.mult).then_inc(S["ema_sq"], 1)
            mods_fix(0)
            scale1(0)
            dve.wait_ge(S["ema_ss"], 1)
            dve.tensor_scalar(ema[:, 2:3], banks[:, 6, 0:1], 1e-24, None, ALU.max).then_inc(S["ema_cl"], 1)
            for b in range(1, B):
                mods_fix(b)
            dve.wait_ge(S["scal_e"], 2)
            chain(dve.tensor_scalar(scal2[:, 4:5], scal2[:, 0:1], -1.0, None, ALU.mult))
            chain(dve.tensor_scalar(scal[:, 1:3], scal2[:, 1:3], 1.0, None, ALU.add))
            chain(dve.reciprocal(scal2[:, 5:7], scal[:, 1:3]))
            dve.tensor_scalar(scal[:, 1:3], scal2[:, 5:7], -1.0, 1.0, ALU.mult, ALU.add).then_inc(S["scal_ok"], 1)
            dve.wait_ge(S["ema_rn"], 1)
            dve.tensor_tensor(ema[:, 1:2], ema[:, 0:1], ema[:, 3:4], ALU.mult).then_inc(S["ema_n"], 1)
            alpha, w_seq, not_alpha, not_w = scal2[:, 5:6], scal2[:, 6:7], scal[:, 1:2], scal[:, 2:3]
            dve.wait_ge(S["scal_ok"], 1)
            dve.wait_ge(S["consts"], 11)

            def router_a(b):
                dve.wait_ge(S["rt_d"], b + 1)
                dve.tensor_tensor(lg[:, :, :], p_logit, rb[:, :].unsqueeze(1).to_broadcast([P, NT, E]), ALU.add)\
                   .then_inc(S["lg_d"], 1)
                dve.wait_ge(S["lg_d"], b + 1)
                dve.tensor_reduce(lmax[:, :], lg[:, :, :], AX.X, ALU.max).then_inc(S["lmax_d"], 1)
                dve.wait_ge(S["lmax_d"], b + 1)
                dve.tensor_tensor(lz[:, :, :], lg[:, :, :], per_exp(lmax[:, :]), ALU.subtract).then_inc(S["lz_d"], 1)
                dve.wait_ge(S["lz_d"], b + 1)
                dve.scalar_tensor_tensor(cand[:, :, :], lz[:, :, :], 0.0, exp_less8[:, :, :], ALU.is_equal, ALU.mult)\
                   .then_inc(S["cand_d"], 1)
                dve.wait_ge(S["cand_d"], b + 1)
                dve.tensor_reduce(cmin[:, :], cand[:, :, :], AX.X, ALU.min).then_inc(S["cmin_d"], 1)
                dve.wait_ge(S["cmin_d"], b + 1)
                dve.tensor_tensor(hot[:, :, :], exp_less8[:, :, :], per_exp(cmin[:, :]), ALU.is_equal).then_inc(S["hot_d"], 1)

            def router_b(b):
                dve.wait_ge(S["lexp_d"], b + 1)
                dve.tensor_reduce(lsum[:, :], lexp[:, :, :], AX.X, ALU.add).then_inc(S["lsum_d"], 1)
                dve.wait_ge(S["lsum_d"], b + 1)
                dve.reciprocal(top[:, :], lsum[:, :]).then_inc(S["top_d"], 1)

            def place(b):
                dve.wait_ge(S["rank_d"], b + 1)
                dve.tensor_tensor(placed[:, :, :], p_rank, exp_base[:, :, :], ALU.add).then_inc(S["pl_d"], 1)
                dve.tensor_reduce(hot_new[:, :], hot[:, :, :].rearrange("p t e -> p e t"), AX.X, ALU.add).then_inc(S["hotn_d"], 1)
                dve.wait_ge(S["pl_d"], b + 1)
                dve.tensor_tensor(placed2[:, :, :], placed[:, :, :], hot[:, :, :], ALU.mult).then_inc(S["pl2_d"], 1)
                dve.wait_ge(S["hotn_d"], b + 1)
                dve.tensor_tensor(hot_sum[:, :], hot_sum[:, :], hot_new[:, :], ALU.add).then_inc(S["hots_d"], 1)
                dve.wait_ge(S["pl2_d"], b + 1)
                dve.tensor_reduce(posf[:, :], placed2[:, :, :], AX.X, ALU.add).then_inc(S["posf_d"], 1)
                dve.wait_ge(S["posf_d"], b + 1)
                wait_for(dve, rows_out[b % 2], 16 * NT * (b // 2))
                dve.tensor_copy(pos2[b % 2][:, :], posf[:, :]).then_inc(S["pos_d"], 1)

            def gelu_in(b):
                dve.wait_ge(S["sq_d"], b + 1)
                wait_for(dve, S["th_d"], b)
                dve.scalar_tensor_tensor(wg[:, :, :], sq[:, :, :], 1.0 / GELU_A, h1[:, :, :], ALU.add, ALU.mult)\
                   .then_inc(S["wg_d"], 1)

            def gelu_out(b):
                dve.wait_ge(S["th_d"], b + 1)
                wait_for(dve, S["og_d"], b)
                wait_for(dve, S["on_d"], b)
                dve.scalar_tensor_tensor(out2[:, :, :], th[:, :, :], 1.0, h1[:, :, :], ALU.add, ALU.mult)\
                   .then_inc(S["out2_d"], 1)

            def norm_clamp(b):
                dve.wait_ge(S["ss_d"], 8 * b + 8)
                wait_for(dve, S["pwn"], b)
                dve.tensor_scalar(ssc[:, :], ss[:, :], 4e-24, None, ALU.max).then_inc(S["ssc_d"], 1)

            def unit(b):
                dve.wait_ge(S["pwn"], b + 1)
                wait_for(dve, S["tr1"], 2 * b)
                dve.tensor_tensor(on[:, :, :], out2[:, :, :], per_tile(rn[:, :]), ALU.mult).then_inc(S["on_d"], 1)

            def stats1(b):
                dve.wait_ge(S["ld_xa"], 16 * b + 16)
                wait_for(dve, S["pw1"], b)
                stats(lambda t: xa[:, t, :], st1, mv1, var1, S["bn1"], S["mv1_d"], S["var1_d"], b, S["nb1"])

            def bias1(b):
                dve.wait_ge(S["pw1"], b + 1)
                wait_for(dve, S["xn1_d"], 8 * b)
                dve.scalar_tensor_tensor(nbias1[:, :], mv1[:, :, 0], -1.0, rstd1[:, :], ALU.mult, ALU.mult)\
                   .then_inc(S["nb1"], 1)

            def nearest(b, tiles):
                for t in tiles:
                    dve.wait_ge(S["sim_d"], 8 * b + t + 1)
                    if t == 0:
                        wait_for(dve, S["fam_d"], b)
                    dve.tensor_reduce(mx[:, t:t + 1], p_sim[t % 2][:, 0:(t + 1) * P], AX.X, ALU.max).then_inc(S["mx_d"], 1)

            def familiarity(b):
                dve.wait_ge(S["ema_d2"], b + 1)
                dve.wait_ge(S["mx_d"], 9 * b + 8)
                dve.tensor_copy(mx[0:1, 0:1], p_ema[0:1, 0:1]).then_inc(S["mx_d"], 1)
                dve.tensor_scalar(fam1[:, :], p_ema, not_w, None, ALU.mult).then_inc(S["fam1_d"], 1)
                dve.wait_ge(S["fam1_d"], b + 1)
                dve.wait_ge(S["mx_d"], 9 * b + 9)
                wait_for(dve, S["nov_d"], b)
                dve.scalar_tensor_tensor(fam[:, :], mx[:, :], w_seq, fam1[:, :], ALU.mult, ALU.add).then_inc(S["fam_d"], 1)

            def residual(b):
                rows = rows2[b % 2]
                dve.wait_ge(S["nov_d"], b + 1)
                dve.tensor_scalar(gate[:, :], nov[:, :], alpha, not_alpha, ALU.mult, ALU.add).then_inc(S["gate_d"], 1)
                dve.wait_ge(S["gate_d"], b + 1)
                dve.wait_ge(S["og_d"], b + 1)
                dve.wait_ge(S["ld_xr"], 16 * b + 16)
                wait_for(dve, rows_out[b % 2], 16 * NT * (b // 2))
                for t in range(NT):
                    dve.scalar_tensor_tensor(rows[:, t, X1:X1 + D], og[:, t, :], gate[:, t:t + 1], xr[:, t, :],
                                             ALU.mult, ALU.add).then_inc(S["x1_d"], 1)
                dve.wait_ge(S["x1_d"], 8 * b + 8)
                wait_for(dve, S["pw2"], b)
                stats(lambda t: rows[:, t, X1:X1 + D], st2, mv2, var2, S["bn2"], S["mv2_d"], S["var2_d"], b, S["nb2"])

            def bias2(b):
                dve.wait_ge(S["pw2"], b + 1)
                wait_for(dve, S["xn2_d"], 8 * b)
                dve.scalar_tensor_tensor(nbias2[:, :], mv2[:, :, 0], -1.0, rstd2[:, :], ALU.mult, ALU.mult).then_inc(S["nb2"], 1)

            def scale2(b):
                dve.wait_ge(S["xn2_d"], 8 * b + 8)
                wait_for(dve, S["h2_d"], b)
                dve.tensor_tensor(hm2[:, :, :], xn2[:, :, :], mod(b, CB), ALU.mult).then_inc(S["hm2_d"], 1)

            gelu_in(0)
            stats1(1)
            gelu_out(0)
            norm_clamp(0)
            bias1(1)
            unit(0)
            scale1(1)
            for b in range(B):
                nxt, old = b + 1 < B, b >= 1
                nearest(b, range(0, 2))
                if nxt:
                    gelu_in(b + 1)
                nearest(b, range(2, 4))
                if nxt:
                    gelu_out(b + 1)
                if old:
                    router_a(b - 1)
                nearest(b, range(4, 6))
                if nxt:
                    norm_clamp(b + 1)
                if old:
                    router_b(b - 1)
                    place(b - 1)
                nearest(b, range(6, 8))
                familiarity(b)
                if nxt:
                    unit(b + 1)
                residual(b)
                if b + 2 < B:
                    stats1(b + 2)
                bias2(b)
                if b + 2 < B:
                    bias1(b + 2)
                scale2(b)
                if b + 2 < B:
                    scale1(b + 2)
            router_a(B - 1)
            router_b(B - 1)
            place(B - 1)

            own = [0]

            def tab(ins):
                own[0] += 1
                ins.then_inc(S["tab_own"], 1)
                dve.wait_ge(S["tab_own"], own[0])

            dve.wait_ge(S["cnt_d"], 1)
            tab(dve.tensor_copy(cnt[:, :], p_count[0:1, :]))
            tab(dve.tensor_tensor(cmp1[:, :, :], cnt[:, :].unsqueeze(2).to_broadcast([1, E, TOKENS // P]), row128[:, :, :], ALU.is_gt))
            tab(dve.tensor_reduce(ntile[:, :], cmp1[:, :, :], AX.X, ALU.add))
            tab(dve.tensor_tensor(cum[:, :, :], upto[:, :, :], ntile[:, :].unsqueeze(1).to_broadcast([1, E, E]), ALU.mult))
            tab(dve.tensor_reduce(tend[:, :], cum[:, :, :], AX.X, ALU.add))
            tab(dve.tensor_tensor(past[:, :, :], tile_no[:, :, :], tend[:, :].unsqueeze(1).to_broadcast([1, TILES, E]), ALU.is_ge))
            tab(dve.tensor_reduce(ek[:, :], past[:, :, :], AX.X, ALU.add))
            tab(dve.tensor_tensor(past_n[:, :, :], past[:, :, :], ntile[:, :].unsqueeze(1).to_broadcast([1, TILES, E]), ALU.mult))
            tab(dve.tensor_reduce(skipped[:, :], past_n[:, :, :], AX.X, ALU.add))
            tab(dve.tensor_tensor(rk[:, :], tile_no[:, :, 0], skipped[:, :], ALU.subtract))
            tab(dve.tensor_scalar(rk2[:, :], rk[:, :], float(P), None, ALU.mult))
            tab(dve.scalar_tensor_tensor(tile_row[:, :], ek[:, :], float(REGION), rk2[:, :], ALU.mult, ALU.add))
            tab(dve.tensor_scalar(tile_exp[:, :], ek[:, :], float(E - 1), None, ALU.min))
            dve.tensor_tensor(pad_at[:, :], cnt[:, :], exp_base[0:1, 0, :], ALU.add).then_inc(S["table_d"], 1)
            dve.wait_ge(S["table_d"], 1)
            dve.wait_ge(S["ld_b"], 32)

            def expert(n):
                return dve.value_load(tile_exp[0:1, n:n + 1] if isinstance(n, int) else tile_exp[0:1, bass.ds(n, 1)],
                                      min_val=0, max_val=E - 1)

            def tile_step(i, j):
                if lives(i, j, 1):
                    n, slot, _ = tile_at(i, j, 1)
                    e = expert(n)
                    dve.wait_ge(S["t_hid"], n + 1)
                    wait_for(dve, S["t_hidT"], n - 1)
                    dve.tensor_tensor(hid[slot % 2][:, :], p_hid[slot % 2], b1[:, bass.ds(e * F, F)], ALU.add)\
                       .then_inc(S["t_hidb"], 1)
                if lives(i, j, 3):
                    n, slot, rnd = tile_at(i, j, 3)
                    e = expert(n)
                    dve.wait_ge(S["t_y"], n + 1)
                    dve.tensor_tensor(y1[:, :], p_y[slot % 2], b2[:, bass.ds(e * D, D)], ALU.add).then_inc(S["t_y1"], 1)
                    dve.wait_ge(S["t_y1"], n + 1)
                    dve.tensor_tensor(y2[:, :], y1[:, :], tb[slot][:, GG:GG + D], ALU.mult).then_inc(S["t_y2"], 1)
                    dve.wait_ge(S["t_y2"], n + 1)
                    wait_for(dve, stored[slot], rnd * 16)
                    dve.tensor_copy(tok[slot][:, :], tb[slot][:, TOK:TOK + 1].bitcast(i32))
                    dve.tensor_tensor(ob[slot][:, :], y2[:, :], tb[slot][:, X1:X1 + D], ALU.add).then_inc(S["t_fin"], 1)
            steps(dve, tile_step)

        @block.tensor
        def _(pe):
            pe.wait_ge(S["consts"], 2)
            pe.wait_ge(S["ld_c"], 16)
            pe.transpose(banks[:, 7, 0:B], c4[:, :], ident[0:B, 0:B]).then_inc(S["c_T"], 1)
            pe.wait_ge(S["c_sil"], 1)
            pe.wait_ge(S["ld_wmod"], 16)
            for b in range(B):
                if b >= 2:
                    pe.wait_ge(S["mod_sb"], b - 1)
                pe.matmul(p_sim[b % 2][:, 0:512], sil_b[:, b, :], wmod[:, 0:512], start=True, stop=True)
                pe.matmul(p_sim[b % 2][:, 512:6 * D], sil_b[:, b, :], wmod[:, 512:6 * D], start=True, stop=True)\
                  .then_inc(S["mod_ps"], 1)
                if b == 0:
                    pe.wait_ge(S["ema_sq"], 1)
                    pe.matmul(banks[:, 6, 0:1], ones[:, :], ema[:, 1:2], start=True, stop=True).then_inc(S["ema_ss"], 1)
            pe.wait_ge(S["consts"], 5)
            pe.wait_ge(S["ema_n"], 1)
            pe.wait_ge(S["mod_sb"], B)
            pe.wait_ge(S["ld_small"], 80)

            def turn(src, b, done, free):
                for t in range(NT):
                    if t % 4 == 0:
                        wait_for(pe, free[0], free[1] + t // 4)
                    ins = pe.transpose(p_turn[:, t * P:(t + 1) * P], src(t), ident[:, :])
                    if t % 4 == 3:
                        ins.then_inc(done, 1)

            def rank(b):
                pe.wait_ge(S["hot_d"], b + 1)
                pe.wait_ge(S["lg_d"], b + 1)
                if b >= 1:
                    pe.wait_ge(S["hots_d"], b)
                pe.matmul(p_rank, before_h[:, :], hot[:, :, :], start=True, stop=False)
                for t in range(NT - 1):
                    n = NT - 1 - t
                    pe.matmul(p_rank[:, t + 1:NT, :], ones_h[:, :], hot[:, t:t + 1, :].to_broadcast([P, n, E]),
                              start=False, stop=False)
                pe.matmul(p_rank, ones_h[:, :], hot_sum[:, :].unsqueeze(1).to_broadcast([P, NT, E]),
                          start=False, stop=True).then_inc(S["rank_d"], 1)

            def turn_on(b):
                pe.wait_ge(S["on_d"], b + 1)
                turn(lambda t: on[:, t, :], b, S["tr1"], (S["h2T_d"], 2 * (b - 2) + 1))

            def turn_h2(b):
                pe.wait_ge(S["h2_d"], b + 1)
                before = (S["onT_d"], 2 * (b + 1) + 1) if b + 1 < B else (S["h2T_d"], 2 * (b - 1) + 1)
                turn(lambda t: rows2[b % 2][:, t, H2:H2 + D], b, S["tr2"], before)

            def sims(b, tiles):
                for t in tiles:
                    if t >= 2:
                        pe.wait_ge(S["mx_d"], 9 * b + t - 1)
                    else:
                        wait_for(pe, S["mx_d"], 9 * (b - 1) + 7 + t)
                    if t % 4 == 0:
                        pe.wait_ge(S["onT_d"], 2 * b + t // 4 + 1)
                    mine = onT[:, t * P:(t + 1) * P]
                    n = (t + 1) * P
                    for c in range(0, n, 512):
                        m = min(512, n - c)
                        last = c + m == n
                        ins = pe.matmul(p_sim[t % 2][:, c:c + m], mine, onT[:, c:c + m], start=True, stop=not last)
                        if last:
                            ins = pe.matmul(p_sim[t % 2][:, n - P:n], ident_h[:, :], mask_h[:, :], start=False, stop=True)
                    ins.then_inc(S["sim_d"], 1)

            def ema_sims(b):
                wait_for(pe, S["fam_d"], b)
                for t in range(NT):
                    ins = pe.matmul(p_ema[:, t:t + 1], onT[:, t * P:(t + 1) * P], ema[:, 1:2], start=True, stop=True)
                ins.then_inc(S["ema_d2"], 1)

            def router(b):
                wait_for(pe, S["pl_d"], b)
                for t in range(NT):
                    if t % 4 == 0:
                        pe.wait_ge(S["h2T_d"], 2 * b + t // 4 + 1)
                    ins = pe.matmul(p_logit[:, t, :], h2T[:, t * P:(t + 1) * P], rw[:, :], start=True, stop=True)
                ins.then_inc(S["rt_d"], 1)

            turn_on(0)
            for b in range(B):
                sims(b, range(0, 2))
                if b >= 1:
                    turn_h2(b - 1)
                sims(b, range(2, 4))
                if b >= 1:
                    router(b - 1)
                sims(b, range(4, 6))
                if b >= 1:
                    rank(b - 1)
                sims(b, range(6, 8))
                ema_sims(b)
                if b + 1 < B:
                    turn_on(b + 1)
            turn_h2(B - 1)
            router(B - 1)
            rank(B - 1)
            pe.wait_ge(S["pl_d"], B)
            pe.wait_ge(S["hots_d"], B)
            pe.matmul(p_count, ones_h[:, :], hot_sum[:, :], start=True, stop=True).then_inc(S["cnt_d"], 1)
            pe.wait_ge(S["table_d"], 1)
            pe.wait_ge(S["ld_w1"], 16)
            pe.wait_ge(S["ld_w2"], 16)

            def expert(n):
                return pe.value_load(tile_exp[0:1, n:n + 1] if isinstance(n, int) else tile_exp[0:1, bass.ds(n, 1)],
                                     min_val=0, max_val=E - 1)

            def tile_step(i, j):
                if lives(i, j, 0):
                    n, slot, rnd = tile_at(i, j, 0)
                    pe.wait_ge(loaded[slot], (rnd + 1) * 16)
                    wait_for(pe, S["t_h2s"], n - 1)
                    pe.transpose(p_h2T[slot % 2], tb[slot][:, H2:H2 + D], ident[:, :]).then_inc(S["t_h2T"], 1)
                if lives(i, j, 1):
                    n, slot, _ = tile_at(i, j, 1)
                    e = expert(n)
                    pe.wait_ge(S["t_h2s"], n + 1)
                    wait_for(pe, S["t_hidb"], n - 1)
                    pe.matmul(p_hid[slot % 2], h2s[slot % 2][:, :], w1[:, bass.ds(e * F, F)], start=True, stop=True)\
                      .then_inc(S["t_hid"], 1)
                if lives(i, j, 2):
                    n, slot, _ = tile_at(i, j, 2)
                    pe.wait_ge(S["t_hidb"], n + 1)
                    wait_for(pe, S["t_hidr"], n - 1)
                    for c in range(FC):
                        ins = pe.transpose(p_hidT[slot % 2][:, c * P:(c + 1) * P], hid[slot % 2][:, c * P:(c + 1) * P], ident[:, :])
                    ins.then_inc(S["t_hidT"], 1)
                if lives(i, j, 3):
                    n, slot, _ = tile_at(i, j, 3)
                    e = expert(n)
                    pe.wait_ge(S["t_hidr"], n + 1)
                    wait_for(pe, S["t_y1"], n - 1)
                    for c in range(FC):
                        ins = pe.matmul(p_y[slot % 2], hidT[slot % 2][:, c * P:(c + 1) * P],
                                        w2[:, bass.ds(e * FC * D + c * D, D)], start=(c == 0), stop=(c == FC - 1))
                    ins.then_inc(S["t_y"], 1)
            steps(pe, tile_step)


_INS = ["L0_attn_x", "L0_attn_ema_out", "L0_attn_logit_decay", "L0_attn_log_tau", "L0_attn_log_blend",
        "L0_attn_logit_blend_seq", "L0_ffn_router_W", "L0_ffn_router_b", "L0_ffn_W1", "L0_ffn_b1", "L0_ffn_W2",
        "L0_ffn_b2", "L0_c", "L0_wmod"]


def kernel(**inputs):
    import numpy as np
    import concourse.bacc as bacc
    from concourse.bass_utils import run_bass_kernel_spmd as run

    nc = bacc.Bacc("TRN2", target_bir_lowering=False, num_devices=1)
    arrays, args = {}, []
    for name in _INS:
        a = np.ascontiguousarray(inputs[name])
        a = a.reshape(a.shape or (1,))
        arrays[f"in_{name}"] = a
        args.append(nc.dram_tensor(f"in_{name}", a.shape, mybir.dt.from_np(a.dtype), kind="ExternalInput").ap())
    args.append(nc.dram_tensor("out_x", (B, T, D), f32, kind="ExternalOutput").ap())
    build(nc, *args)
    return run(nc, [arrays], core_ids=[0]).results[0]["out_x"]
```

```python
import concourse.bass as bass
from concourse import mybir
from contextlib import ExitStack

f32, bf16, i32 = mybir.dt.float32, mybir.dt.bfloat16, mybir.dt.int32
ALU = mybir.AluOpType
ACT = mybir.ActivationFunctionType
AX = mybir.AxisListType

B, T, D = 4, 1024, 128
P = 128
NT = T // P
H = NT // 2
HALVES = 2 * B
GROUPS = [((2 * b, 2 * b + 1), 2 * b + 3) for b in range(B - 1)] + [((HALVES - 2,), HALVES), ((HALVES - 1,), HALVES + 1)]
RING = 6
E, F = 8, 512
FC = F // P
TOKENS = B * T
TILES = (TOKENS + E * (P - 1)) // P
REGION = TOKENS + P
DUMMY = TILES - TOKENS // P
H2, X1, GG, TOK = 0, D, 2 * D, 3 * D
ROW = 3 * D + 4
LN_EPS = 1e-5
GELU_A = 0.044715
GELU_C = 0.7978845608028654
MASKED = -4.0
SLOTS = 6
WINDOWS, WINDOW = TILES // SLOTS + 1, SLOTS + 2
SA, CA, GA, SB, CB, GB = range(6)
MOD_PARTS = ((0, 2), (2, 6))
WARM = 10
CONSTS = 13


def wait_for(eng, sem, value):
    if not (isinstance(value, int) and value <= 0):
        eng.wait_ge(sem, value)


def build(nc, x_d, ema_d, decay_d, tau_d, blend_d, seq_d, rw_d, rb_d, w1_d, b1_d, w2_d, b2_d, c_d, wmod_d, out_d):
    ctx = ExitStack()
    with ctx:
        def sb(name, shape, dt=f32):
            return ctx.enter_context(nc.sbuf_tensor(name, shape, dt))

        def sem(name):
            return ctx.enter_context(nc.semaphore(name))

        rows_d = nc.dram_tensor("expert_rows", [E * REGION + DUMMY * P, ROW], f32, kind="Internal").ap()
        out_rows = out_d.rearrange("b t d -> (b t) d")

        ident = sb("ident", [P, P])
        ident_h = sb("ident_h", [P, P], bf16)
        mask_h = sb("mask_h", [P, P], bf16)
        before_h = sb("before_h", [P, P], bf16)
        ones_h = sb("ones_h", [P, P], bf16)
        ones = sb("ones", [P, P])
        minus_half = sb("minus_half", [P, H])
        exp_less8 = sb("exp_less8", [P, NT, E])
        exp_base = sb("exp_base", [P, NT, E])
        row128 = sb("row128", [1, E, TOKENS // P])
        upto = sb("upto", [1, E, E])
        tile_no = sb("tile_no", [1, WINDOWS * WINDOW])
        tok_no = sb("tok_no", [P, B * NT], i32)
        pad_row = sb("pad_row", [P, ROW])
        w1 = sb("w1", [P, E * F])
        w2 = sb("w2", [P, E * FC * D])
        b1_rows = sb("b1_rows", [E * FC, P])
        b1 = sb("b1", [P, E * FC])
        b2 = sb("b2", [P, E * D])
        rw = sb("rw", [P, E])
        rb = sb("rb", [P, E])
        wmod = sb("wmod", [P, 6 * D])
        mods = sb("mods", [P, B, 6, D])
        c4 = sb("c4", [B, D])
        sil = sb("sil", [P, 4, B])
        mod4 = sb("mod4", [B, 6, D])
        pick = sb("pick", [B, B, P])
        ema = sb("ema", [P, 4])
        scal = sb("scal", [P, 3])
        scal2 = sb("scal2", [P, 8])
        gsign = sb("gsign", [B, 2, D])
        gabs = sb("gabs", [B, 2, D])
        gmag = sb("gmag", [B, 2, D])

        xa = sb("xa", [P, NT, D])
        xr = sb("xr", [P, NT, D])
        st1 = sb("st1", [P, NT, 6])
        mv1 = sb("mv1", [P, NT, 2])
        var1 = sb("var1", [P, NT])
        rstd1 = sb("rstd1", [P, NT])
        nbias1 = sb("nbias1", [P, NT])
        xn1 = sb("xn1", [P, NT, D])
        hm1 = sb("hm1", [P, NT, D])
        h1 = sb("h1", [P, NT, D])
        sq = sb("sq", [P, NT, D])
        wg = sb("wg", [P, NT, D])
        th = sb("th", [P, NT, D])
        out2 = sb("out2", [P, NT, D])
        og = sb("og", [P, NT, D])
        junk = sb("junk", [P, NT, D])
        ss = sb("ss", [P, NT])
        ssc = sb("ssc", [P, NT])
        rn = sb("rn", [P, NT])
        on = sb("on", [P, NT, D])
        onT2 = [sb(f"onT{i}", [P, T]) for i in range(2)]
        mx = sb("mx", [P, NT])
        fam1 = sb("fam1", [P, H])
        fam = sb("fam", [P, NT])
        nov = sb("nov", [P, NT])
        gate = sb("gate", [P, NT])
        rows_ring = [sb(f"rows{i}", [P, H, ROW]) for i in range(RING)]
        st2 = sb("st2", [P, NT, 6])
        mv2 = sb("mv2", [P, NT, 2])
        var2 = sb("var2", [P, NT])
        rstd2 = sb("rstd2", [P, NT])
        nbias2 = sb("nbias2", [P, NT])
        xn2 = sb("xn2", [P, NT, D])
        hm2 = sb("hm2", [P, NT, D])
        h2T = sb("h2T", [P, T])
        lg = sb("lg", [P, NT, E])
        lmax = sb("lmax", [P, NT])
        lz = sb("lz", [P, NT, E])
        lexp = sb("lexp", [P, NT, E])
        lsum = sb("lsum", [P, NT])
        top = sb("top", [P, NT])
        cand = sb("cand", [P, NT, E])
        cmin = sb("cmin", [P, NT])
        hot = sb("hot", [P, NT, E], bf16)
        hot_new = sb("hot_new", [P, E])
        hot_sum = sb("hot_sum", [P, E], bf16)
        placed = sb("placed", [P, NT, E])
        placed2 = sb("placed2", [P, NT, E])
        posf = sb("posf", [P, NT])
        pos_ring = [sb(f"pos{i}", [P, NT], i32) for i in range(3)]

        cnt = sb("cnt", [1, E])
        cmp1 = sb("cmp1", [1, E, TOKENS // P])
        ntile = sb("ntile", [1, E])
        cum = sb("cum", [1, E, E])
        tend = sb("tend", [1, E])
        past = sb("past", [1, WINDOWS * WINDOW, E])
        past_n = sb("past_n", [1, WINDOWS * WINDOW, E])
        ek = sb("ek", [1, WINDOWS * WINDOW])
        skipped = sb("skipped", [1, WINDOWS * WINDOW])
        rk = sb("rk", [1, WINDOWS * WINDOW])
        rk2 = sb("rk2", [1, WINDOWS * WINDOW])
        tile_exp = sb("tile_exp", [1, WINDOWS * WINDOW], i32)
        tile_row = sb("tile_row", [1, WINDOWS * WINDOW], i32)
        pad_at = sb("pad_at", [1, E], i32)

        tb = [sb(f"tb{s}", [P, ROW]) for s in range(SLOTS)]
        ob = [sb(f"ob{s}", [P, D]) for s in range(SLOTS)]
        tok = [sb(f"tok{s}", [P, 1], i32) for s in range(SLOTS)]
        h2s = [sb(f"h2s{s}", [P, P]) for s in range(2)]
        w1s = [sb(f"w1s{s}", [P, F]) for s in range(2)]
        hidb = [sb(f"hidb{s}", [P, F]) for s in range(2)]
        hid = [sb(f"hid{s}", [P, F]) for s in range(2)]
        y1 = sb("y1", [P, D])
        y2 = sb("y2", [P, D])

        banks = ctx.enter_context(nc.psum_tensor("banks", [P, 8, 512], f32))
        p_on = banks[:, 0, :]
        p_h2 = banks[:, 1, :]
        p_sim = [banks[:, 2:4, :].rearrange("p a n -> p (a n)"), banks[:, 4:6, :].rearrange("p a n -> p (a n)")]
        p_mod4 = p_sim[0][0:B, 0:6 * D]
        p_ema = banks[:, 6, 0:H]
        p_logit = banks[:, 7, 0:NT * E].rearrange("p (t e) -> p t e", e=E)
        p_rank = banks[:, 7, NT * E:2 * NT * E].rearrange("p (t e) -> p t e", e=E)
        p_count = banks[:, 7, 0:E]
        p_b1 = banks[:, 7, 2 * NT * E:2 * NT * E + E * FC]
        p_h2T = [banks[:, a, 0:P] for a in (0, 1)]
        p_hid = [banks[:, a, :] for a in (2, 3)]
        p_y = [banks[:, a, 0:D] for a in (6, 7)]

        names = """ld_c ld_wmod ld_small ld_ema ld_w1 ld_w2 ld_b ld_b1 dummy_out pads_out b1_T b1_ok
            pool_own consts ema_sq ema_ss ema_cl ema_rn ema_n c_T c_exp c_sil mod_raw mod4_ok mod_ps mod_sb
            scal_e scal_ok dve_prep
            bn1 mv1_d var1_d pw1 nb1 xn1_d hm1_d h1_d sq_d wg_d th_d out2_d og_d ss_d ssc_d pwn on_d
            tr1 onT_d ema_d2 sim_d mx_d mx0_d fam1_d fam_d nov_d gate_d x1_d bn2 mv2_d var2_d pw2 nb2 xn2_d hm2_d h2_d
            tr2 h2T_d rt_d lg_d lmax_d lz_d lexp_d lsum_d top_d cand_d cmin_d hot_d rank_d hotn_d hots_d pl_d pl2_d posf_d pos_d
            gg_d cnt_d tab_own table_d
            t_h2T t_h2s t_w1s t_hid t_hidb t_hidr t_y t_y1 t_y2 t_fin put_turn""".split()
        S = {n: sem(n) for n in names}
        ld_xa = [sem(f"ld_xa{i}") for i in range(2)]
        ld_xr = [sem(f"ld_xr{i}") for i in range(2)]
        rows_out = [sem(f"rows_out{i}") for i in range(RING)]
        loaded = [sem(f"loaded{s}") for s in range(SLOTS)]
        stored = [sem(f"stored{s}") for s in range(SLOTS)]

        block = ctx.enter_context(nc.Block())

        def mod(u, which):
            return mods[:, u // 2, which:which + 1, :].to_broadcast([P, H, D])

        def mods_of(eng, u):
            eng.wait_ge(S["mod_sb"], 2 * (u // 2) + 2)

        def half(buf, u):
            a = H * (u % 2)
            return buf[:, a:a + H, :] if len(buf.shape) == 3 else buf[:, a:a + H]

        def half_x(u):
            return x_d[u // 2][T // 2 * (u % 2):T // 2 * (u % 2 + 1)].rearrange("(t p) d -> p t d", p=P)

        def of_value(col, n):
            return col.unsqueeze(2).to_broadcast([P, col.shape[1], n])

        def run_at(u, work):
            if 0 <= u < HALVES:
                work(u)

        def router_at(m, work):
            for g, (units, at) in enumerate(GROUPS):
                if at == m:
                    work(g)

        def group_of(u):
            return next((g, H * units.index(u)) for g, (units, _) in enumerate(GROUPS) if u in units)

        def tiles_of(g):
            return H * len(GROUPS[g][0])

        def tile_at(i, j, d):
            q = 2 + j - d
            return 6 * i + q, q % SLOTS, i + q // SLOTS

        def steps(eng, step, table=None):
            def window(i):
                if table is None:
                    return None
                at = table[0:1, i * WINDOW:i * WINDOW + WINDOW] if isinstance(i, int) else \
                    table[0:1, bass.ds(i * WINDOW, WINDOW)]
                _, values = nc.values_load_multi_w_load_instructions(
                    at, engines=[eng.engine], min_val=0, max_val=E - 1,
                    skip_runtime_bounds_check_because="the table is clamped to the experts on chip")
                return values

            first = window(0)
            for j in range(4, SLOTS):
                step(-1, j, lambda d: first[2 + j - d - SLOTS])
            for j in range(SLOTS):
                step(0, j, lambda d: first[2 + j - d])
            with eng.Fori(1, (TILES - 3) // SLOTS) as i:
                now = window(i)
                for j in range(SLOTS):
                    step(i, j, lambda d: now[2 + j - d])
            last = window((TILES - 3) // SLOTS)
            for j in range(3):
                step((TILES - 3) // SLOTS, j, lambda d: last[2 + j - d])

        def lives(i, j, d):
            n = tile_at(i, j, d)[0]
            return not isinstance(n, int) or 0 <= n < TILES

        @block.sync
        def _(sp):
            sp.dma_start(c4[:, :], c_d).then_inc(S["ld_c"], 16)

            def load_xa(u):
                if u >= 2:
                    sp.wait_ge(S["xn1_d"], u - 1)
                sp.dma_start(half(xa, u), half_x(u)).then_inc(ld_xa[u % 2], 16)

            def load_xr(u):
                if u >= 2:
                    sp.wait_ge(S["x1_d"], u - 1)
                sp.dma_start(half(xr, u), half_x(u)).then_inc(ld_xr[u % 2], 16)

            load_xa(0)
            sp.dma_start(wmod[:, :], wmod_d).then_inc(S["ld_wmod"], 16)
            load_xa(1)
            load_xr(0)
            load_xr(1)
            sp.wait_ge(S["consts"], CONSTS)
            sp.dma_start(rows_d[E * REGION:E * REGION + DUMMY * P, :].rearrange("(j p) c -> p j c", p=P),
                         pad_row[:, :].unsqueeze(1).to_broadcast([P, DUMMY, ROW])).then_inc(S["dummy_out"], 16)
            load_xa(2)
            load_xa(3)
            for u in range(2, HALVES):
                if u + 2 < HALVES:
                    load_xa(u + 2)
                load_xr(u)

            def rows_of(i):
                at = tile_row[0:1, i * WINDOW:i * WINDOW + WINDOW] if isinstance(i, int) else \
                    tile_row[0:1, bass.ds(i * WINDOW, WINDOW)]
                _, values = nc.values_load_multi_w_load_instructions(
                    at, engines=[sp.engine], min_val=0, max_val=E * REGION + (DUMMY - 1) * P,
                    skip_runtime_bounds_check_because="a tile's rows lie in a region whatever the counts are")
                return values

            sp.wait_ge(S["table_d"], 1)
            _, pads = nc.values_load_multi_w_load_instructions(
                pad_at[0:1, :], engines=[sp.engine], min_val=0, max_val=E * REGION - P,
                skip_runtime_bounds_check_because="an expert has at most all tokens")
            for e in range(E):
                sp.dma_start(rows_d[bass.ds(pads[e], P), :], pad_row[:, :]).then_inc(S["pads_out"], 16)
            at = rows_of(0)
            for n, q in enumerate(rows_out):
                sp.wait_ge(q, 16 * H * len(range(n, HALVES, RING)))
            sp.wait_ge(S["pads_out"], 16 * E)
            sp.wait_ge(S["dummy_out"], 16)

            def load(i, slot, at):
                if not isinstance(i, int) or i > 0:
                    sp.wait_ge(S["t_fin"], (i - 1) * SLOTS + slot + 1)
                sp.dma_start(tb[slot][:, :], rows_d[bass.ds(at[slot], P), :]).then_inc(loaded[slot], 16)

            for slot in range(SLOTS):
                load(0, slot, at)
            with sp.Fori(1, TILES // SLOTS) as i:
                at = rows_of(i)
                for slot in range(SLOTS):
                    load(i, slot, at)
            at = rows_of(TILES // SLOTS)
            for slot in range(TILES % SLOTS):
                load(TILES // SLOTS, slot, at)
            for slot in range(SLOTS):
                sp.wait_ge(stored[slot], 16 * ((TILES - 1 - slot) // SLOTS + 1))

        @block.gpsimd
        def _(pool):
            own = [0]

            def chain(ins):
                own[0] += 1
                ins.then_inc(S["pool_own"], 1)
                pool.wait_ge(S["pool_own"], own[0])

            def const(ins):
                ins.then_inc(S["consts"], 1)

            chain(pool.memset(ident[:, :], 0.0))
            const(pool.affine_select(out=ident[:, :], in_=ident[:, :], compare_op=ALU.not_equal, fill=1.0, base=0,
                                     pattern=[[-1, P]], channel_multiplier=1))
            pool.memset(minus_half[:, :], -0.5)
            chain(pool.memset(pick[:, :, :], 0.0))
            const(pool.affine_select(out=pick[:, :, :], in_=pick[:, :, :], compare_op=ALU.not_equal, fill=1.0, base=0,
                                     pattern=[[-1, B], [0, P]], channel_multiplier=1))
            const(pool.memset(ones[:, :], 1.0))
            pool.memset(ident_h[:, :], 0.0)
            pool.memset(mask_h[:, :], 0.0)
            pool.memset(before_h[:, :], 1.0)
            pool.memset(pad_row[:, :], 0.0)
            pool.memset(upto[:, :, :], 1.0)
            pool.memset(ones_h[:, :], 1.0)
            for rows in rows_ring:
                pool.memset(rows[:, :, TOK + 1:ROW], 0.0)
            chain(pool.memset(hot_sum[:, :], 0.0))
            const(pool.affine_select(out=ident_h[:, :], in_=ident_h[:, :], compare_op=ALU.not_equal, fill=1.0, base=0,
                                     pattern=[[-1, P]], channel_multiplier=1))
            const(pool.affine_select(out=mask_h[:, :], in_=mask_h[:, :], compare_op=ALU.is_gt, fill=MASKED, base=0,
                                     pattern=[[-1, P]], channel_multiplier=1))
            const(pool.affine_select(out=before_h[:, :], in_=before_h[:, :], compare_op=ALU.is_gt, fill=0.0, base=0,
                                     pattern=[[1, P]], channel_multiplier=-1))
            const(pool.affine_select(out=upto[:, :, :], in_=upto[:, :, :], compare_op=ALU.is_ge, fill=0.0, base=0,
                                     pattern=[[1, E], [-1, E]], channel_multiplier=0))
            const(pool.memset(pad_row[:, TOK:TOK + 1].bitcast(i32), 1 << 20))
            big = dict(channel_multiplier=0, base=0, allow_small_or_imprecise_dtypes=True)
            const(pool.iota(exp_less8[:, :, :], [[0, NT], [1, E]], **{**big, "base": -E}))
            const(pool.iota(exp_base[:, :, :], [[0, NT], [REGION, E]], **big))
            const(pool.iota(row128[:, :, :], [[0, E], [P, TOKENS // P]], **big))
            const(pool.iota(tile_no[:, :], [[SLOTS, WINDOWS], [1, WINDOW]], **big))
            const(pool.iota(tok_no[:, :], [[P, B * NT]], base=0, channel_multiplier=1))

            def pow_half(out, in_, done):
                pool.tensor_tensor(out, in_, minus_half[:, 0:in_.shape[1]], ALU.pow).then_inc(done, 1)

            def rstd1_of(u):
                pool.wait_ge(S["var1_d"], u + 1)
                wait_for(pool, S["xn1_d"], u - 1)
                pow_half(half(rstd1, u), half(var1, u), S["pw1"])

            def rstd2_of(u):
                pool.wait_ge(S["var2_d"], u + 1)
                wait_for(pool, S["xn2_d"], u - 1)
                pow_half(half(rstd2, u), half(var2, u), S["pw2"])

            def shift1(u):
                pool.wait_ge(S["hm1_d"], u + 1)
                wait_for(pool, S["out2_d"], u - 1)
                pool.tensor_tensor(half(h1, u), half(hm1, u), mod(u, SA), ALU.add).then_inc(S["h1_d"], 1)

            def shift2(u):
                pool.wait_ge(S["hm2_d"], u + 1)
                pool.tensor_tensor(rows_ring[u % RING][:, :, H2:H2 + D], half(hm2, u), mod(u, SB), ALU.add).then_inc(S["h2_d"], 1)

            def norm_pow(u):
                pool.wait_ge(S["ssc_d"], u + 1)
                wait_for(pool, S["on_d"], u - 1)
                pow_half(half(rn, u), half(ssc, u), S["pwn"])

            def gated(u):
                pool.wait_ge(S["out2_d"], u + 1)
                mods_of(pool, u)
                wait_for(pool, S["x1_d"], u - 1)
                pool.tensor_tensor(half(og, u), half(out2, u), mod(u, GA), ALU.mult).then_inc(S["og_d"], 1)

            def scatter(u, tiles):
                if tiles[0] == 0:
                    pool.wait_ge(S["gg_d"], u + 1)
                    pool.wait_ge(S["h2_d"], u + 1)
                    pool.wait_ge(S["pos_d"], group_of(u)[0] + 1)
                for t in tiles:
                    at = group_of(u)[1] + t
                    pool.indirect_dma_start(rows_d[:, :],
                                            bass.IndirectOffsetOnAxis(ap=pos_ring[group_of(u)[0] % 3][:, at:at + 1], axis=0),
                                            rows_ring[u % RING][:, t, :], None).then_inc(rows_out[u % RING], 16)

            rstd1_of(0)
            shift1(0)
            pool.wait_ge(S["ema_cl"], 1)
            pow_half(ema[:, 3:4], ema[:, 2:3], S["ema_rn"])
            rstd1_of(1)
            for m in range(-1, HALVES):
                run_at(m - 4, lambda u: scatter(u, range(0, 3)))
                run_at(m + 1, gated)
                run_at(m + 1, norm_pow)
                run_at(m - 1, shift2)
                run_at(m + 2, shift1)
                run_at(m, rstd2_of)
                run_at(m - 4, lambda u: scatter(u, range(3, 4)))
                run_at(m + 3, rstd1_of)
            scatter(HALVES - 4, range(0, 2))
            shift2(HALVES - 1)
            scatter(HALVES - 4, range(2, 4))
            for u in range(HALVES - 3, HALVES):
                scatter(u, range(H))

            last_row = pool.snap(TOKENS - 1)

            def put(i, j, _):
                if not lives(i, j, 2):
                    return
                n, slot, rnd = tile_at(i, j, 2)
                pool.wait_ge(S["t_fin"], n + 1)
                pool.sem_inc(S["put_turn"], 1)
                pool.indirect_dma_start(out_rows, bass.IndirectOffsetOnAxis(ap=tok[slot][:, :], axis=0),
                                        ob[slot][:, :], None, bounds_check=last_row, oob_is_err=False)\
                    .then_inc(stored[slot], 16)
            steps(pool, put)

        @block.scalar
        def _(act):
            act.dma_start(ema[:, 0:1], ema_d.unsqueeze(1)).then_inc(S["ld_ema"], 16)
            act.wait_ge(S["c_T"], 1)
            act.activation(sil[:, 0, :], banks[:, 7, 0:B], ACT.Exp, scale=-1.0).then_inc(S["c_exp"], 1)
            act.dma_start(scal[:, 0:1], tau_d.unsqueeze(0).to_broadcast([P, 1])).then_inc(S["ld_small"], 16)
            act.dma_start(scal[:, 1:2], blend_d.unsqueeze(0).to_broadcast([P, 1])).then_inc(S["ld_small"], 16)
            act.dma_start(scal[:, 2:3], seq_d.unsqueeze(0).to_broadcast([P, 1])).then_inc(S["ld_small"], 16)
            act.dma_start(rw[:, :], rw_d).then_inc(S["ld_small"], 16)
            act.dma_start(b1_rows[:, :], b1_d.rearrange("e (c p) -> (e c) p", p=P)).then_inc(S["ld_b1"], 16)
            act.dma_start(rb[:, :], rb_d.unsqueeze(0).to_broadcast([P, E])).then_inc(S["ld_small"], 16)
            def normed(u, src, out, rstd, nbias, done):
                for t in range(H):
                    at = H * (u % 2) + t
                    ins = act.activation(out[:, at, :], src(t), ACT.Identity, bias=nbias[:, at:at + 1], scale=rstd[:, at:at + 1])
                ins.then_inc(done, 1)

            def normed1(u):
                act.wait_ge(S["nb1"], u + 1)
                wait_for(act, S["hm1_d"], u - 1)
                normed(u, lambda t: xa[:, H * (u % 2) + t, :], xn1, rstd1, nbias1, S["xn1_d"])

            def normed2(u):
                act.wait_ge(S["nb2"], u + 1)
                wait_for(act, S["hm2_d"], u - 1)
                normed(u, lambda t: rows_ring[u % RING][:, t, X1:X1 + D], xn2, rstd2, nbias2, S["xn2_d"])

            def mods_out(b, part):
                first, last = MOD_PARTS[part]
                act.wait_ge(S["mod_ps"], 2 * b + part + 1)
                act.activation(mods[:, b, first:last, :].rearrange("p a d -> p (a d)"),
                               p_sim[(b + 1) % 2][:, 512 * part:512 * part + (last - first) * D], ACT.Copy).then_inc(S["mod_sb"], 1)

            def square(u):
                act.wait_ge(S["h1_d"], u + 1)
                wait_for(act, S["wg_d"], u - 1)
                act.activation(half(sq, u), half(h1, u), ACT.Square).then_inc(S["sq_d"], 1)

            def tanh(u):
                act.wait_ge(S["wg_d"], u + 1)
                wait_for(act, S["out2_d"], u - 1)
                act.activation(half(th, u), half(wg, u), ACT.Tanh, scale=GELU_C * GELU_A).then_inc(S["th_d"], 1)

            def norms(u):
                act.wait_ge(S["out2_d"], u + 1)
                wait_for(act, S["ssc_d"], u - 1)
                for t in range(H):
                    at = H * (u % 2) + t
                    ins = act.activation(junk[:, at, :], out2[:, at, :], ACT.Square, accum_out=ss[:, at:at + 1])
                ins.then_inc(S["ss_d"], 1)

            def novelty(u):
                act.wait_ge(S["fam_d"], u + 1)
                wait_for(act, S["gate_d"], u - 1)
                act.activation(half(nov, u), half(fam, u), ACT.Exp, scale=scal2[:, 4:5]).then_inc(S["nov_d"], 1)

            def onT_out(u):
                act.wait_ge(S["tr1"], u + 1)
                wait_for(act, S["ema_d2"], 2 * (u // 2) - 2)
                a = T // 2 * (u % 2)
                act.activation(onT2[u // 2 % 2][:, a:a + T // 2], p_on, ACT.Copy).then_inc(S["onT_d"], 1)

            def h2T_out(u):
                act.wait_ge(S["tr2"], u + 1)
                if u >= 2:
                    act.wait_ge(S["rt_d"], group_of(u - 2)[0] + 1)
                a = T // 2 * (u % 2)
                act.activation(h2T[:, a:a + T // 2], p_h2, ACT.Copy).then_inc(S["h2T_d"], 1)

            def router_exp(g):
                act.wait_ge(S["lz_d"], g + 1)
                n = tiles_of(g)
                act.activation(lexp[:, 0:n, :], lz[:, 0:n, :], ACT.Exp).then_inc(S["lexp_d"], 1)

            def row_gates(u):
                g, first = group_of(u)
                act.wait_ge(S["top_d"], g + 1)
                mods_of(act, u)
                src = mods[:, u // 2, GB, :]
                rows = rows_ring[u % RING]
                wait_for(act, rows_out[u % RING], 16 * H * (u // RING))
                for t in range(H):
                    act.activation(rows[:, t, GG:GG + D], src, ACT.Copy, scale=top[:, first + t:first + t + 1])
                toks = tok_no[:, u * H:u * H + H]
                act.activation(rows[:, :, TOK:TOK + 1].bitcast(i32).squeeze(2), toks, ACT.Copy).then_inc(S["gg_d"], 1)

            normed1(0)
            mods_out(0, 0)
            mods_out(0, 1)
            act.wait_ge(S["ld_small"], 80)
            act.activation(scal2[:, 0:1], scal[:, 0:1], ACT.Exp).then_inc(S["scal_e"], 1)
            act.activation(scal2[:, 1:3], scal[:, 1:3], ACT.Exp, scale=-1.0).then_inc(S["scal_e"], 1)
            square(0)
            act.dma_start(w1[:, :].rearrange("p (e f) -> p e f", e=E), w1_d.rearrange("e d f -> d e f")).then_inc(S["ld_w1"], 16)
            act.dma_start(w2[:, :].rearrange("p (e c d) -> p e c d", e=E, c=FC),
                          w2_d.rearrange("e (c p) d -> p e c d", p=P)).then_inc(S["ld_w2"], 16)
            act.dma_start(b2[:, :], b2_d.rearrange("e d -> (e d)").unsqueeze(0).to_broadcast([P, E * D])).then_inc(S["ld_b"], 16)
            for m in range(-1, HALVES):
                run_at(m - 1, normed2)
                run_at(m + 1, tanh)
                if m == -1:
                    mods_out(1, 0)
                    mods_out(1, 1)
                run_at(m + 2, normed1)
                run_at(m + 1, norms)
                if m == -1:
                    mods_out(2, 0)
                    mods_out(2, 1)
                run_at(m, novelty)
                if m == -1:
                    mods_out(3, 0)
                    mods_out(3, 1)
                    act.wait_ge(S["scal_ok"], 1)
                if m == 0:
                    act.wait_ge(S["b1_T"], 1)
                    act.activation(b1[:, :], p_b1, ACT.Copy).then_inc(S["b1_ok"], 1)
                run_at(m + 1, onT_out)
                run_at(m + 2, square)
                run_at(m - 1, h2T_out)
                if m % 2 == 0:
                    run_at(m - 3, row_gates)
                router_at(m, router_exp)
                if m % 2 == 1:
                    run_at(m - 3, row_gates)
            normed2(HALVES - 1)
            router_exp(len(GROUPS) - 2)
            row_gates(HALVES - 3)
            h2T_out(HALVES - 1)
            row_gates(HALVES - 2)
            router_exp(len(GROUPS) - 1)
            row_gates(HALVES - 1)

            act.wait_ge(S["table_d"], 1)
            act.wait_ge(S["ld_w1"], 16)

            def tile_step(i, j, expert):
                if lives(i, j, 0):
                    n, slot, _ = tile_at(i, j, 0)
                    wait_for(act, S["t_hid"], n - 1)
                    act.activation(w1s[slot % 2][:, :], w1[:, bass.ds(expert(0) * F, F)], ACT.Copy).then_inc(S["t_w1s"], 1)
                    act.wait_ge(S["t_h2T"], n + 1)
                    act.activation(h2s[slot % 2][:, :], p_h2T[slot % 2], ACT.Copy).then_inc(S["t_h2s"], 1)
                if lives(i, j, 1):
                    n, slot, _ = tile_at(i, j, 1)
                    act.wait_ge(S["t_hidb"], n + 1)
                    wait_for(act, S["t_y"], n - 1)
                    act.activation(hid[slot % 2][:, :], hidb[slot % 2][:, :], ACT.Relu).then_inc(S["t_hidr"], 1)
            steps(act, tile_step, tile_exp)

        @block.vector
        def _(dve):
            prep = [0]

            def chain(ins):
                prep[0] += 1
                ins.then_inc(S["dve_prep"], 1)
                dve.wait_ge(S["dve_prep"], prep[0])

            def stats(u, src, st, mv, var, done_bn, done_mv, done_var, used):
                for t in range(H):
                    ins = dve.bn_stats(st[:, H * (u % 2) + t, :], src(t))
                ins.then_inc(done_bn, 1)
                dve.wait_ge(done_bn, u + 1)
                wait_for(dve, used, u - 1)
                for t in range(H):
                    at = H * (u % 2) + t
                    ins = dve.bn_aggr(mv[:, at, :], st[:, at, :])
                ins.then_inc(done_mv, 1)
                dve.wait_ge(done_mv, u + 1)
                dve.tensor_scalar(half(var, u), half(mv, u)[:, :, 1], LN_EPS, None, ALU.add).then_inc(done_var, 1)

            def stats1(u):
                dve.wait_ge(ld_xa[u % 2], 16 * (u // 2) + 16)
                wait_for(dve, S["pw1"], u - 1)
                stats(u, lambda t: xa[:, H * (u % 2) + t, :], st1, mv1, var1, S["bn1"], S["mv1_d"], S["var1_d"], S["nb1"])

            def bias1(u):
                dve.wait_ge(S["pw1"], u + 1)
                wait_for(dve, S["xn1_d"], u - 1)
                dve.scalar_tensor_tensor(half(nbias1, u), half(mv1, u)[:, :, 0], -1.0, half(rstd1, u), ALU.mult, ALU.mult)\
                   .then_inc(S["nb1"], 1)

            def scale1(u):
                dve.wait_ge(S["xn1_d"], u + 1)
                dve.wait_ge(S["mod_sb"], 2 * (u // 2) + 1)
                wait_for(dve, S["h1_d"], u - 1)
                dve.tensor_tensor(half(hm1, u), half(xn1, u), mod(u, CA), ALU.mult).then_inc(S["hm1_d"], 1)

            def gelu_in(u):
                dve.wait_ge(S["sq_d"], u + 1)
                wait_for(dve, S["th_d"], u - 1)
                dve.scalar_tensor_tensor(half(wg, u), half(sq, u), 1.0 / GELU_A, half(h1, u), ALU.add, ALU.mult)\
                   .then_inc(S["wg_d"], 1)

            def gelu_out(u):
                dve.wait_ge(S["th_d"], u + 1)
                wait_for(dve, S["og_d"], u - 1)
                wait_for(dve, S["on_d"], u - 1)
                dve.scalar_tensor_tensor(half(out2, u), half(th, u), 1.0, half(h1, u), ALU.add, ALU.mult)\
                   .then_inc(S["out2_d"], 1)

            def norm_clamp(u):
                dve.wait_ge(S["ss_d"], u + 1)
                wait_for(dve, S["pwn"], u - 1)
                dve.tensor_scalar(half(ssc, u), half(ss, u), 4e-24, None, ALU.max).then_inc(S["ssc_d"], 1)

            def unit(u):
                dve.wait_ge(S["pwn"], u + 1)
                wait_for(dve, S["tr1"], u - 1)
                dve.tensor_tensor(half(on, u), half(out2, u), of_value(half(rn, u), D), ALU.mult).then_inc(S["on_d"], 1)

            def nearest(u, t):
                dve.wait_ge(S["sim_d"], H * u + t + 1)
                at = H * (u % 2) + t
                if t == 0:
                    wait_for(dve, S["fam_d"], u - 1)
                dve.tensor_reduce(mx[:, at:at + 1], p_sim[t % 2][:, 0:(at + 1) * P], AX.X, ALU.max).then_inc(S["mx_d"], 1)

            def familiarity(u):
                dve.wait_ge(S["ema_d2"], u + 1)
                dve.wait_ge(S["mx_d"], H * u + H)
                if u % 2 == 0:
                    dve.tensor_copy(mx[0:1, 0:1], p_ema[0:1, 0:1]).then_inc(S["mx0_d"], 1)
                dve.tensor_scalar(fam1[:, :], p_ema, not_w, None, ALU.mult).then_inc(S["fam1_d"], 1)
                dve.wait_ge(S["fam1_d"], u + 1)
                dve.wait_ge(S["mx0_d"], u // 2 + 1)
                wait_for(dve, S["nov_d"], u - 1)
                dve.scalar_tensor_tensor(half(fam, u), half(mx, u), w_seq, fam1[:, :], ALU.mult, ALU.add).then_inc(S["fam_d"], 1)

            def residual(u):
                rows = rows_ring[u % RING]
                dve.wait_ge(S["nov_d"], u + 1)
                dve.tensor_scalar(half(gate, u), half(nov, u), alpha, not_alpha, ALU.mult, ALU.add).then_inc(S["gate_d"], 1)
                dve.wait_ge(S["gate_d"], u + 1)
                dve.wait_ge(S["og_d"], u + 1)
                dve.wait_ge(ld_xr[u % 2], 16 * (u // 2) + 16)
                wait_for(dve, rows_out[u % RING], 16 * H * (u // RING))
                for t in range(H):
                    at = H * (u % 2) + t
                    ins = dve.scalar_tensor_tensor(rows[:, t, X1:X1 + D], og[:, at, :], gate[:, at:at + 1], xr[:, at, :],
                                                   ALU.mult, ALU.add)
                ins.then_inc(S["x1_d"], 1)

            def stats2(u):
                dve.wait_ge(S["x1_d"], u + 1)
                wait_for(dve, S["pw2"], u - 1)
                stats(u, lambda t: rows_ring[u % RING][:, t, X1:X1 + D], st2, mv2, var2,
                      S["bn2"], S["mv2_d"], S["var2_d"], S["nb2"])

            def bias2(u):
                dve.wait_ge(S["pw2"], u + 1)
                wait_for(dve, S["xn2_d"], u - 1)
                dve.scalar_tensor_tensor(half(nbias2, u), half(mv2, u)[:, :, 0], -1.0, half(rstd2, u), ALU.mult, ALU.mult)\
                   .then_inc(S["nb2"], 1)

            def scale2(u):
                dve.wait_ge(S["xn2_d"], u + 1)
                dve.wait_ge(S["mod_sb"], 2 * (u // 2) + 2)
                wait_for(dve, S["h2_d"], u - 1)
                dve.tensor_tensor(half(hm2, u), half(xn2, u), mod(u, CB), ALU.mult).then_inc(S["hm2_d"], 1)

            def router_a(g):
                n = tiles_of(g)
                dve.wait_ge(S["rt_d"], g + 1)
                dve.tensor_tensor(lg[:, 0:n, :], p_logit[:, 0:n, :], rb[:, :].unsqueeze(1).to_broadcast([P, n, E]), ALU.add)\
                   .then_inc(S["lg_d"], 1)
                dve.wait_ge(S["lg_d"], g + 1)
                dve.tensor_reduce(lmax[:, 0:n], lg[:, 0:n, :], AX.X, ALU.max).then_inc(S["lmax_d"], 1)
                dve.wait_ge(S["lmax_d"], g + 1)
                dve.tensor_tensor(lz[:, 0:n, :], lg[:, 0:n, :], of_value(lmax[:, 0:n], E), ALU.subtract).then_inc(S["lz_d"], 1)
                dve.wait_ge(S["lz_d"], g + 1)
                dve.scalar_tensor_tensor(cand[:, 0:n, :], lz[:, 0:n, :], 0.0, exp_less8[:, 0:n, :], ALU.is_equal, ALU.mult)\
                   .then_inc(S["cand_d"], 1)
                dve.wait_ge(S["cand_d"], g + 1)
                dve.tensor_reduce(cmin[:, 0:n], cand[:, 0:n, :], AX.X, ALU.min).then_inc(S["cmin_d"], 1)
                dve.wait_ge(S["cmin_d"], g + 1)
                dve.tensor_tensor(hot[:, 0:n, :], exp_less8[:, 0:n, :], of_value(cmin[:, 0:n], E), ALU.is_equal).then_inc(S["hot_d"], 1)

            def router_b(g):
                n = tiles_of(g)
                dve.wait_ge(S["lexp_d"], g + 1)
                dve.tensor_reduce(lsum[:, 0:n], lexp[:, 0:n, :], AX.X, ALU.add).then_inc(S["lsum_d"], 1)
                dve.wait_ge(S["lsum_d"], g + 1)
                wait_for(dve, S["gg_d"], GROUPS[g][0][0])
                dve.reciprocal(top[:, 0:n], lsum[:, 0:n]).then_inc(S["top_d"], 1)

            def place(g):
                n = tiles_of(g)
                dve.wait_ge(S["rank_d"], g + 1)
                dve.tensor_tensor(placed[:, 0:n, :], p_rank[:, 0:n, :], exp_base[:, 0:n, :], ALU.add).then_inc(S["pl_d"], 1)
                dve.tensor_reduce(hot_new[:, :], hot[:, 0:n, :].rearrange("p t e -> p e t"), AX.X, ALU.add).then_inc(S["hotn_d"], 1)
                dve.wait_ge(S["pl_d"], g + 1)
                dve.tensor_tensor(placed2[:, 0:n, :], placed[:, 0:n, :], hot[:, 0:n, :], ALU.mult).then_inc(S["pl2_d"], 1)
                dve.wait_ge(S["hotn_d"], g + 1)
                dve.tensor_tensor(hot_sum[:, :], hot_sum[:, :], hot_new[:, :], ALU.add).then_inc(S["hots_d"], 1)
                dve.wait_ge(S["pl2_d"], g + 1)
                dve.tensor_reduce(posf[:, 0:n], placed2[:, 0:n, :], AX.X, ALU.add).then_inc(S["posf_d"], 1)
                dve.wait_ge(S["posf_d"], g + 1)
                if g >= 3:
                    for u in GROUPS[g - 3][0]:
                        dve.wait_ge(rows_out[u % RING], 16 * H * (u // RING + 1))
                dve.tensor_copy(pos_ring[g % 3][:, 0:n], posf[:, 0:n]).then_inc(S["pos_d"], 1)

            dve.wait_ge(S["c_exp"], 1)
            chain(dve.tensor_scalar(sil[:, 1, :], sil[:, 0, :], 1.0, None, ALU.add))
            chain(dve.reciprocal(sil[:, 2, :], sil[:, 1, :]))
            dve.tensor_tensor(sil[:, 3, :], sil[:, 2, :], banks[:, 7, 0:B], ALU.mult).then_inc(S["c_sil"], 1)
            stats1(0)

            dve.wait_ge(S["mod_raw"], 1)
            raw = p_mod4.rearrange("b (a d) -> b a d", a=6)
            dve.tensor_copy(mod4[:, SA::3, :], raw[:, SA::3, :])
            dve.tensor_scalar(mod4[:, CA::3, :], raw[:, CA::3, :], 1.0, None, ALU.add).then_inc(S["mod4_ok"], 1)
            bias1(0)
            chain(dve.tensor_copy(mod4[:, GA::3, :], raw[:, GA::3, :]))
            g = mod4[:, GA::3, :]
            dve.tensor_scalar(gsign[:, :, :], g, 0.0, 2.0, ALU.is_ge, ALU.mult)
            chain(dve.scalar_tensor_tensor(gabs[:, :, :], g, -1.0, g, ALU.mult, ALU.max))
            dve.tensor_scalar(gmag[:, 0, :], gabs[:, 0, :], 0.25, 0.5, ALU.max, ALU.mult)
            chain(dve.tensor_scalar(gmag[:, 1, :], gabs[:, 1, :], 0.25, None, ALU.max))
            dve.scalar_tensor_tensor(g, gsign[:, :, :], -1.0, gmag[:, :, :], ALU.add, ALU.mult).then_inc(S["mod4_ok"], 1)
            dve.wait_ge(S["ld_ema"], 16)
            dve.tensor_tensor(ema[:, 1:2], ema[:, 0:1], ema[:, 0:1], ALU.mult).then_inc(S["ema_sq"], 1)
            scale1(0)
            dve.wait_ge(S["ema_ss"], 1)
            dve.tensor_scalar(ema[:, 2:3], banks[:, 6, 0:1], 1e-24, None, ALU.max).then_inc(S["ema_cl"], 1)
            stats1(1)
            dve.wait_ge(S["scal_e"], 2)
            chain(dve.tensor_scalar(scal2[:, 4:5], scal2[:, 0:1], -1.0, None, ALU.mult))
            chain(dve.tensor_scalar(scal[:, 1:3], scal2[:, 1:3], 1.0, None, ALU.add))
            chain(dve.reciprocal(scal2[:, 5:7], scal[:, 1:3]))
            dve.tensor_scalar(scal[:, 1:3], scal2[:, 5:7], -1.0, 1.0, ALU.mult, ALU.add).then_inc(S["scal_ok"], 1)
            dve.wait_ge(S["ema_rn"], 1)
            dve.tensor_tensor(ema[:, 1:2], ema[:, 0:1], ema[:, 3:4], ALU.mult).then_inc(S["ema_n"], 1)
            alpha, w_seq, not_alpha, not_w = scal2[:, 5:6], scal2[:, 6:7], scal[:, 1:2], scal[:, 2:3]
            dve.wait_ge(S["scal_ok"], 1)
            dve.wait_ge(S["consts"], CONSTS)
            chain(dve.tensor_scalar(tile_no[:, :], tile_no[:, :], float(TILES - 1), None, ALU.min))

            for m in range(-1, HALVES):
                run_at(m, lambda u: nearest(u, 0))
                router_at(m - 1, place)
                run_at(m - 1, bias2)
                run_at(m + 2, bias1)
                run_at(m, lambda u: nearest(u, 1))
                run_at(m + 1, gelu_in)
                run_at(m, lambda u: nearest(u, 2))
                run_at(m + 1, gelu_out)
                run_at(m, lambda u: nearest(u, 3))
                run_at(m, familiarity)
                run_at(m + 1, norm_clamp)
                run_at(m - 1, scale2)
                run_at(m, residual)
                run_at(m + 1, unit)
                run_at(m + 2, scale1)
                router_at(m, router_a)
                run_at(m, stats2)
                run_at(m + 3, stats1)
                router_at(m, router_b)
            router_at(HALVES - 1, place)
            bias2(HALVES - 1)
            router_a(len(GROUPS) - 2)
            scale2(HALVES - 1)
            router_b(len(GROUPS) - 2)
            place(len(GROUPS) - 2)
            router_a(len(GROUPS) - 1)
            router_b(len(GROUPS) - 1)
            place(len(GROUPS) - 1)

            own = [0]

            def tab(ins):
                own[0] += 1
                ins.then_inc(S["tab_own"], 1)
                dve.wait_ge(S["tab_own"], own[0])

            dve.wait_ge(S["cnt_d"], 1)
            tab(dve.tensor_copy(cnt[:, :], p_count[0:1, :]))
            tab(dve.tensor_tensor(cmp1[:, :, :], cnt[:, :].unsqueeze(2).to_broadcast([1, E, TOKENS // P]), row128[:, :, :], ALU.is_gt))
            tab(dve.tensor_reduce(ntile[:, :], cmp1[:, :, :], AX.X, ALU.add))
            tab(dve.tensor_tensor(cum[:, :, :], upto[:, :, :], ntile[:, :].unsqueeze(1).to_broadcast([1, E, E]), ALU.mult))
            tab(dve.tensor_reduce(tend[:, :], cum[:, :, :], AX.X, ALU.add))
            tab(dve.tensor_tensor(past[:, :, :], tile_no[:, :].unsqueeze(2).to_broadcast([1, WINDOWS * WINDOW, E]),
                                  tend[:, :].unsqueeze(1).to_broadcast([1, WINDOWS * WINDOW, E]), ALU.is_ge))
            tab(dve.tensor_reduce(ek[:, :], past[:, :, :], AX.X, ALU.add))
            tab(dve.tensor_tensor(past_n[:, :, :], past[:, :, :], ntile[:, :].unsqueeze(1).to_broadcast([1, WINDOWS * WINDOW, E]), ALU.mult))
            tab(dve.tensor_reduce(skipped[:, :], past_n[:, :, :], AX.X, ALU.add))
            tab(dve.tensor_tensor(rk[:, :], tile_no[:, :], skipped[:, :], ALU.subtract))
            tab(dve.tensor_scalar(rk2[:, :], rk[:, :], float(P), None, ALU.mult))
            tab(dve.scalar_tensor_tensor(tile_row[:, :], ek[:, :], float(REGION), rk2[:, :], ALU.mult, ALU.add))
            tab(dve.tensor_scalar(tile_exp[:, :], ek[:, :], float(E - 1), None, ALU.min))
            dve.tensor_tensor(pad_at[:, :], cnt[:, :], exp_base[0:1, 0, :], ALU.add).then_inc(S["table_d"], 1)
            dve.wait_ge(S["table_d"], 1)
            dve.wait_ge(S["ld_b"], 16)
            dve.wait_ge(S["b1_ok"], 1)

            def tile_step(i, j, expert):
                if lives(i, j, 1):
                    n, slot, _ = tile_at(i, j, 1)
                    dve.wait_ge(S["t_hid"], n + 1)
                    wait_for(dve, S["t_hidr"], n - 1)
                    bias = b1[:, bass.ds(expert(1) * FC, FC)].unsqueeze(2).to_broadcast([P, FC, P])
                    dve.tensor_tensor(hidb[slot % 2][:, :].rearrange("p (c n) -> p c n", c=FC),
                                      p_hid[slot % 2].rearrange("p (c n) -> p c n", c=FC), bias, ALU.add)\
                       .then_inc(S["t_hidb"], 1)
                if lives(i, j, 2):
                    n, slot, rnd = tile_at(i, j, 2)
                    dve.wait_ge(S["t_y"], n + 1)
                    dve.tensor_tensor(y1[:, :], p_y[slot % 2], b2[:, bass.ds(expert(2) * D, D)], ALU.add).then_inc(S["t_y1"], 1)
                    wait_for(dve, stored[slot], rnd * 16)
                    dve.tensor_copy(tok[slot][:, :], tb[slot][:, TOK:TOK + 1].bitcast(i32))
                    dve.wait_ge(S["t_y1"], n + 1)
                    dve.tensor_tensor(y2[:, :], y1[:, :], tb[slot][:, GG:GG + D], ALU.mult).then_inc(S["t_y2"], 1)
                    dve.wait_ge(S["t_y2"], n + 1)
                    dve.tensor_tensor(ob[slot][:, :], y2[:, :], tb[slot][:, X1:X1 + D], ALU.add).then_inc(S["t_fin"], 1)
            steps(dve, tile_step, tile_exp)

        @block.tensor
        def _(pe):
            pe.wait_ge(S["consts"], 1)
            pe.wait_ge(S["ld_c"], 16)
            pe.transpose(banks[:, 7, 0:B], c4[:, :], ident[0:B, 0:B]).then_inc(S["c_T"], 1)
            pe.wait_ge(S["c_sil"], 1)
            pe.wait_ge(S["ld_wmod"], 16)
            pe.matmul(p_mod4[:, 0:512], sil[:, 3, :], wmod[:, 0:512], start=True, stop=True)
            pe.matmul(p_mod4[:, 512:6 * D], sil[:, 3, :], wmod[:, 512:6 * D], start=True, stop=True).then_inc(S["mod_raw"], 1)

            def spread(b, part):
                first, last = MOD_PARTS[part]
                pe.matmul(p_sim[(b + 1) % 2][:, 512 * part:512 * part + (last - first) * D], pick[:, b, :],
                          mod4[:, first:last, :].rearrange("b a d -> b (a d)"), start=True, stop=True).then_inc(S["mod_ps"], 1)

            pe.wait_ge(S["consts"], 3)
            pe.wait_ge(S["mod4_ok"], 1)
            spread(0, 0)
            pe.wait_ge(S["mod4_ok"], 2)
            spread(0, 1)
            pe.wait_ge(S["ema_sq"], 1)
            pe.matmul(banks[:, 6, 0:1], ones[:, :], ema[:, 1:2], start=True, stop=True).then_inc(S["ema_ss"], 1)
            for b in range(1, B):
                for part in range(2):
                    if b >= 2:
                        pe.wait_ge(S["mod_sb"], 2 * (b - 2) + part + 1)
                    spread(b, part)
            pe.wait_ge(S["ld_b1"], 16)
            pe.transpose(p_b1, b1_rows[:, :], ident[0:E * FC, 0:E * FC]).then_inc(S["b1_T"], 1)
            pe.wait_ge(S["consts"], 6)
            pe.wait_ge(S["ema_n"], 1)
            pe.wait_ge(S["ld_small"], 80)

            def keep_warm(_):
                for _ in range(WARM):
                    pe.matmul(p_on, ones_h[:, :], ones_h[:, :].unsqueeze(1).to_broadcast([P, H, P]), start=True, stop=True)

            def turn_on(u):
                pe.wait_ge(S["on_d"], u + 1)
                wait_for(pe, S["onT_d"], u)
                for t in range(H):
                    ins = pe.transpose(p_on[:, t * P:(t + 1) * P], on[:, H * (u % 2) + t, :], ident[:, :])
                ins.then_inc(S["tr1"], 1)

            def turn_h2(u):
                pe.wait_ge(S["h2_d"], u + 1)
                wait_for(pe, S["h2T_d"], u)
                for t in range(H):
                    ins = pe.transpose(p_h2[:, t * P:(t + 1) * P], rows_ring[u % RING][:, t, H2:H2 + D], ident[:, :])
                ins.then_inc(S["tr2"], 1)

            def sims(u):
                onT = onT2[u // 2 % 2]
                for t in range(H):
                    wait_for(pe, S["mx_d"], H * u + t - 1)
                    if t == 0:
                        pe.wait_ge(S["onT_d"], u + 1)
                        if u == 0:
                            pe.wait_ge(S["mod_sb"], 2 * B)
                    at = H * (u % 2) + t
                    mine = onT[:, at * P:(at + 1) * P]
                    n = (at + 1) * P
                    for c in range(0, n, 512):
                        w = min(512, n - c)
                        last = c + w == n
                        ins = pe.matmul(p_sim[t % 2][:, c:c + w], mine, onT[:, c:c + w], start=True, stop=not last)
                        if last:
                            ins = pe.matmul(p_sim[t % 2][:, n - P:n], ident_h[:, :], mask_h[:, :], start=False, stop=True)
                    ins.then_inc(S["sim_d"], 1)

            def ema_sims(u):
                wait_for(pe, S["fam_d"], u)
                a = T // 2 * (u % 2)
                for t in range(H):
                    ins = pe.matmul(p_ema[:, t:t + 1], onT2[u // 2 % 2][:, a + t * P:a + (t + 1) * P], ema[:, 1:2],
                                    start=True, stop=True)
                ins.then_inc(S["ema_d2"], 1)

            def router(g):
                wait_for(pe, S["pl_d"], g)
                if g == 0:
                    pe.wait_ge(S["b1_ok"], 1)
                for n, u in enumerate(GROUPS[g][0]):
                    pe.wait_ge(S["h2T_d"], u + 1)
                    for t in range(H):
                        at = H * (u % 2) + t
                        ins = pe.matmul(p_logit[:, H * n + t, :], h2T[:, at * P:(at + 1) * P], rw[:, :], start=True, stop=True)
                ins.then_inc(S["rt_d"], 1)

            def rank(g):
                pe.wait_ge(S["hot_d"], g + 1)
                wait_for(pe, S["hots_d"], g)
                n = tiles_of(g)
                pe.matmul(p_rank[:, 0:n, :], before_h[:, :], hot[:, 0:n, :], start=True, stop=False)
                for t in range(n - 1):
                    pe.matmul(p_rank[:, t + 1:n, :], ones_h[:, :], hot[:, t:t + 1, :].to_broadcast([P, n - 1 - t, E]),
                              start=False, stop=False)
                pe.matmul(p_rank[:, 0:n, :], ones_h[:, :], hot_sum[:, :].unsqueeze(1).to_broadcast([P, n, E]),
                          start=False, stop=True).then_inc(S["rank_d"], 1)

            for m in range(-1, HALVES):
                run_at(m, sims)
                run_at(m, ema_sims)
                router_at(m, router)
                run_at(m, keep_warm)
                run_at(m + 1, turn_on)
                run_at(m - 1, turn_h2)
                router_at(m, rank)
            router(len(GROUPS) - 2)
            rank(len(GROUPS) - 2)
            keep_warm(HALVES)
            turn_h2(HALVES - 1)
            router(len(GROUPS) - 1)
            rank(len(GROUPS) - 1)
            pe.wait_ge(S["pl_d"], len(GROUPS))
            pe.wait_ge(S["hots_d"], len(GROUPS))
            pe.matmul(p_count, ones_h[:, :], hot_sum[:, :], start=True, stop=True).then_inc(S["cnt_d"], 1)
            pe.wait_ge(S["table_d"], 1)
            pe.wait_ge(S["ld_w1"], 16)
            pe.wait_ge(S["ld_w2"], 16)

            def tile_step(i, j, expert):
                if lives(i, j, 0):
                    n, slot, rnd = tile_at(i, j, 0)
                    pe.wait_ge(loaded[slot], (rnd + 1) * 16)
                    wait_for(pe, S["t_h2s"], n - 1)
                    pe.transpose(p_h2T[slot % 2], tb[slot][:, H2:H2 + D], ident[:, :]).then_inc(S["t_h2T"], 1)
                if lives(i, j, 1):
                    n, slot, _ = tile_at(i, j, 1)
                    pe.wait_ge(S["t_w1s"], n + 1)
                    pe.wait_ge(S["t_h2s"], n + 1)
                    wait_for(pe, S["t_hidb"], n - 1)
                    for c in range(FC):
                        ins = pe.matmul(p_hid[slot % 2][:, c * P:(c + 1) * P], w1s[slot % 2][:, c * P:(c + 1) * P],
                                        h2s[slot % 2][:, :], start=True, stop=True)
                    ins.then_inc(S["t_hid"], 1)
                if lives(i, j, 2):
                    n, slot, _ = tile_at(i, j, 2)
                    pe.wait_ge(S["t_hidr"], n + 1)
                    wait_for(pe, S["t_y1"], n - 1)
                    for c in range(FC):
                        ins = pe.matmul(p_y[slot % 2], hid[slot % 2][:, c * P:(c + 1) * P],
                                        w2[:, bass.ds(expert(2) * (FC * D) + c * D, D)], start=(c == 0), stop=(c == FC - 1))
                    ins.then_inc(S["t_y"], 1)
            steps(pe, tile_step, tile_exp)


_INS = ["L0_attn_x", "L0_attn_ema_out", "L0_attn_logit_decay", "L0_attn_log_tau", "L0_attn_log_blend",
        "L0_attn_logit_blend_seq", "L0_ffn_router_W", "L0_ffn_router_b", "L0_ffn_W1", "L0_ffn_b1", "L0_ffn_W2",
        "L0_ffn_b2", "L0_c", "L0_wmod"]


def kernel(**inputs):
    import numpy as np
    import concourse.bacc as bacc
    from concourse.bass_utils import run_bass_kernel_spmd as run

    nc = bacc.Bacc("TRN2", target_bir_lowering=False, num_devices=1)
    arrays, args = {}, []
    for name in _INS:
        a = np.ascontiguousarray(inputs[name])
        a = a.reshape(a.shape or (1,))
        arrays[f"in_{name}"] = a
        args.append(nc.dram_tensor(f"in_{name}", a.shape, mybir.dt.from_np(a.dtype), kind="ExternalInput").ap())
    args.append(nc.dram_tensor("out_x", (B, T, D), f32, kind="ExternalOutput").ap())
    build(nc, *args)
    return run(nc, [arrays], core_ids=[0]).results[0]["out_x"]
```

```python
import concourse.bass as bass
from concourse import mybir
from contextlib import ExitStack

f32, bf16, i32 = mybir.dt.float32, mybir.dt.bfloat16, mybir.dt.int32
ALU = mybir.AluOpType
ACT = mybir.ActivationFunctionType
AX = mybir.AxisListType

B, T, D = 4, 1024, 128
P = 128
NT = T // P
H = NT // 2
HALVES = 2 * B
GROUPS = [((u, u + 1), u + 3) for u in range(0, HALVES // 2, 2)] + [((u,), u + 2) for u in range(HALVES // 2, HALVES)]
RING = 6
E, F = 8, 512
FC = F // P
TOKENS = B * T
TILES = (TOKENS + E * (P - 1)) // P
REGION = TOKENS + P
DUMMY = TILES - TOKENS // P
H2, X1, GG, TOK = 0, D, 2 * D, 3 * D
ROW = 3 * D + 4
LN_EPS = 1e-5
GELU_A = 0.044715
GELU_C = 0.7978845608028654
MASKED = -4.0
SLOTS = 6
WINDOWS, WINDOW = TILES // SLOTS + 1, SLOTS + 2
EARLY = (TOKENS // 2 - E * (P - 1)) // P
LATE = (WINDOWS - 1) * WINDOW
assert EARLY == WINDOW
SA, CA, GA, SB, CB, GB = range(6)
MOD_PARTS = ((0, 2), (2, 6))
WARM = (12, 6)
CONSTS = 15


def wait_for(eng, sem, value):
    if not (isinstance(value, int) and value <= 0):
        eng.wait_ge(sem, value)


def build(nc, x_d, ema_d, decay_d, tau_d, blend_d, seq_d, rw_d, rb_d, w1_d, b1_d, w2_d, b2_d, c_d, wmod_d, out_d):
    ctx = ExitStack()
    with ctx:
        def sb(name, shape, dt=f32):
            return ctx.enter_context(nc.sbuf_tensor(name, shape, dt))

        def sem(name):
            return ctx.enter_context(nc.semaphore(name))

        rows_d = nc.dram_tensor("expert_rows", [E * REGION + DUMMY * P, ROW], f32, kind="Internal").ap()
        out_rows = out_d.rearrange("b t d -> (b t) d")

        ident = sb("ident", [P, P])
        ident_h = sb("ident_h", [P, P], bf16)
        mask_h = sb("mask_h", [P, P], bf16)
        before_h = sb("before_h", [P, P], bf16)
        ones_h = sb("ones_h", [P, P], bf16)
        ones = sb("ones", [P, P])
        minus_half = sb("minus_half", [P, H])
        exp_less8 = sb("exp_less8", [P, NT, E])
        exp_base = sb("exp_base", [P, NT, E])
        row128 = sb("row128", [1, E, TOKENS // P])
        upto = sb("upto", [1, E, E])
        early_no = sb("early_no", [1, EARLY])
        tile_no = sb("tile_no", [1, LATE])
        tok_no = sb("tok_no", [P, B * NT], i32)
        pad_row = sb("pad_row", [P, ROW])
        w1 = sb("w1", [P, E * F])
        w2 = sb("w2", [P, E * FC * D])
        b1_rows = sb("b1_rows", [E * FC, P])
        b1 = sb("b1", [P, E * FC])
        b2 = sb("b2", [P, E * D])
        rw = sb("rw", [P, E])
        rb = sb("rb", [P, E])
        wmod = sb("wmod", [P, 6 * D])
        mods = sb("mods", [P, B, 6, D])
        c4 = sb("c4", [B, D])
        sil = sb("sil", [P, 4, B])
        mod4 = sb("mod4", [B, 6, D])
        pick = sb("pick", [B, B, P])
        ema = sb("ema", [P, 4])
        ema_n = sb("ema_n", [P, 2])
        scal = sb("scal", [P, 3])
        scal2 = sb("scal2", [P, 8])
        gsign = sb("gsign", [B, 2, D])
        gabs = sb("gabs", [B, 2, D])
        gmag = sb("gmag", [B, 2, D])

        xa = sb("xa", [P, NT, D])
        xr = sb("xr", [P, NT, D])
        st1 = sb("st1", [P, NT, 6])
        mv1 = sb("mv1", [P, NT, 2])
        var1 = sb("var1", [P, NT])
        rstd1 = sb("rstd1", [P, NT])
        nbias1 = sb("nbias1", [P, NT])
        xn1 = sb("xn1", [P, NT, D])
        hm1 = sb("hm1", [P, NT, D])
        h1 = sb("h1", [P, NT, D])
        sq = sb("sq", [P, NT, D])
        wg = sb("wg", [P, NT, D])
        th = sb("th", [P, NT, D])
        out2 = sb("out2", [P, NT, D])
        og = sb("og", [P, NT, D])
        junk = sb("junk", [P, NT, D])
        ss = sb("ss", [P, NT])
        ssc = sb("ssc", [P, NT])
        rn = sb("rn", [P, NT])
        on = sb("on", [P, NT, D])
        onT2 = [sb(f"onT{i}", [P, T]) for i in range(2)]
        mx = sb("mx", [P, NT])
        fam = sb("fam", [P, NT])
        nov = sb("nov", [P, NT])
        gate = sb("gate", [P, NT])
        rows_ring = [sb(f"rows{i}", [P, H, ROW]) for i in range(RING)]
        st2 = sb("st2", [P, NT, 6])
        mv2 = sb("mv2", [P, NT, 2])
        var2 = sb("var2", [P, NT])
        rstd2 = sb("rstd2", [P, NT])
        nbias2 = sb("nbias2", [P, NT])
        xn2 = sb("xn2", [P, NT, D])
        hm2 = sb("hm2", [P, NT, D])
        h2T = sb("h2T", [P, T])
        lg = sb("lg", [P, NT, E])
        lmax = sb("lmax", [P, NT])
        lz = sb("lz", [P, NT, E])
        lexp = sb("lexp", [P, NT, E])
        lsum = sb("lsum", [P, NT])
        top = sb("top", [P, NT])
        cand = sb("cand", [P, NT, E])
        cmin = sb("cmin", [P, NT])
        hot = sb("hot", [P, NT, E], bf16)
        hot_new = sb("hot_new", [P, E])
        hot_sum = sb("hot_sum", [P, E], bf16)
        placed = sb("placed", [P, NT, E])
        placed2 = sb("placed2", [P, NT, E])
        posf = sb("posf", [P, NT])
        pos_ring = [sb(f"pos{i}", [P, NT], i32) for i in range(3)]

        cnt = sb("cnt", [1, E])
        cmp1 = sb("cmp1", [1, E, TOKENS // P])
        ntile = sb("ntile", [1, E])
        cum = sb("cum", [1, E, E])
        tend = sb("tend", [1, E])
        past = sb("past", [1, LATE, E])
        past_n = sb("past_n", [1, LATE, E])
        ek = sb("ek", [1, LATE])
        skipped = sb("skipped", [1, LATE])
        rk = sb("rk", [1, LATE])
        rk2 = sb("rk2", [1, LATE])
        tile_exp = sb("tile_exp", [1, WINDOWS * WINDOW], i32)
        tile_row = sb("tile_row", [1, WINDOWS * WINDOW], i32)
        left = sb("left", [1, E])
        beside = sb("beside", [1, E])
        cnt0 = sb("cnt0", [1, E])
        cmp0 = sb("cmp0", [1, E, TOKENS // 2 // P])
        full = sb("full", [1, E])
        cum0 = sb("cum0", [1, E, E])
        fend = sb("fend", [1, E])
        past0 = sb("past0", [1, EARLY, E])
        past0_n = sb("past0_n", [1, EARLY, E])
        ek0 = sb("ek0", [1, EARLY])
        skipped0 = sb("skipped0", [1, EARLY])
        rk0 = sb("rk0", [1, EARLY])
        rk02 = sb("rk02", [1, EARLY])
        room = sb("room", [1, E])
        room2 = sb("room2", [1, E])
        done = sb("done", [1, E + 1])
        pad_at = sb("pad_at", [1, E], i32)

        tb = [sb(f"tb{s}", [P, ROW]) for s in range(SLOTS)]
        ob = [sb(f"ob{s}", [P, D]) for s in range(SLOTS)]
        tok = [sb(f"tok{s}", [P, 1], i32) for s in range(SLOTS)]
        h2s = [sb(f"h2s{s}", [P, P]) for s in range(2)]
        w1s = [sb(f"w1s{s}", [P, F]) for s in range(2)]
        hidb = [sb(f"hidb{s}", [P, F]) for s in range(2)]
        hid = [sb(f"hid{s}", [P, F]) for s in range(2)]
        y1 = sb("y1", [P, D])
        y2 = sb("y2", [P, D])

        banks = ctx.enter_context(nc.psum_tensor("banks", [P, 8, 512], f32))
        p_on = banks[:, 0, :]
        p_h2 = banks[:, 1, :]
        p_sim = [banks[:, 2:4, :].rearrange("p a n -> p (a n)"), banks[:, 4:6, :].rearrange("p a n -> p (a n)")]
        p_mod4 = p_sim[0][0:B, 0:6 * D]
        p_ema = banks[:, 6, 0:2 * H].rearrange("p (t n) -> p t n", n=2)
        p_logit = banks[:, 7, 0:NT * E].rearrange("p (t e) -> p t e", e=E)
        p_rank = banks[:, 7, NT * E:2 * NT * E].rearrange("p (t e) -> p t e", e=E)
        p_count = banks[:, 7, 3 * NT * E:3 * NT * E + E]
        p_b1 = banks[:, 7, 2 * NT * E:2 * NT * E + E * FC]
        p_h2T = [banks[:, a, 0:P] for a in (0, 6)]
        p_hid = [banks[:, a, :] for a in (2, 3)]
        p_y = [banks[:, a, 0:D] for a in (4, 5)]

        names = """ld_c ld_wmod ld_small ld_ema ld_w1 ld_w2 ld_b ld_b1 dummy_out pads_out b1_T b1_ok
            pool_own consts ema_sq ema_ss ema_cl ema_rn ema_n c_T c_exp c_sil mod_raw mod4_ok mod_ps mod_sb
            scal_e scal_ok dve_prep
            bn1 mv1_d var1_d pw1 nb1 xn1_d hm1_d h1_d sq_d wg_d th_d out2_d og_d ss_d ssc_d pwn on_d
            tr1 onT_d ema_d2 sim_d mx_d mx0_d fam_d nov_d gate_d x1_d bn2 mv2_d var2_d pw2 nb2 xn2_d hm2_d h2_d
            tr2 h2T_d rt_d lg_d lmax_d lz_d lexp_d lsum_d top_d cand_d cmin_d hot_d rank_d hotn_d hots_d pl_d pl2_d posf_d pos_d
            gg_d cnt0_d cnt0_ok tab0_own table0_d cnt_d pad_at_d tab_own table_d
            t_h2T t_h2s t_w1s t_hid t_hidb t_hidr t_y t_y1 t_y2 t_fin put_turn""".split()
        S = {n: sem(n) for n in names}
        ld_xa = [sem(f"ld_xa{i}") for i in range(2)]
        ld_xr = [sem(f"ld_xr{i}") for i in range(2)]
        rows_out = [sem(f"rows_out{i}") for i in range(RING)]
        loaded = [sem(f"loaded{s}") for s in range(SLOTS)]
        stored = [sem(f"stored{s}") for s in range(SLOTS)]

        block = ctx.enter_context(nc.Block())

        def mod(u, which):
            return mods[:, u // 2, which:which + 1, :].to_broadcast([P, H, D])

        def mods_of(eng, u):
            eng.wait_ge(S["mod_sb"], 2 * (u // 2) + 2)

        def half(buf, u):
            a = H * (u % 2)
            return buf[:, a:a + H, :] if len(buf.shape) == 3 else buf[:, a:a + H]

        def half_x(u):
            return x_d[u // 2][T // 2 * (u % 2):T // 2 * (u % 2 + 1)].rearrange("(t p) d -> p t d", p=P)

        def of_value(col, n):
            return col.unsqueeze(2).to_broadcast([P, col.shape[1], n])

        def run_at(u, work):
            if 0 <= u < HALVES:
                work(u)

        def router_at(m, work):
            for g, (units, at) in enumerate(GROUPS):
                if at == m:
                    work(g)

        def group_of(u):
            return next((g, H * units.index(u)) for g, (units, _) in enumerate(GROUPS) if u in units)

        def tiles_of(g):
            return H * len(GROUPS[g][0])

        def tile_at(i, j, d):
            q = 2 + j - d
            return 6 * i + q, q % SLOTS, i + q // SLOTS

        def window(eng, table, i):
            at = table[0:1, i * WINDOW:i * WINDOW + WINDOW] if isinstance(i, int) else \
                table[0:1, bass.ds(i * WINDOW, WINDOW)]
            top = E - 1 if table is tile_exp else E * REGION + (DUMMY - 1) * P
            _, values = nc.values_load_multi_w_load_instructions(
                at, engines=[eng.engine], min_val=0, max_val=top,
                skip_runtime_bounds_check_because="the table is made on chip within these bounds whatever the counts are")
            return values

        def early_steps(eng, step):
            eng.wait_ge(S["table0_d"], 1)
            first = window(eng, tile_exp, 0)
            return lambda s: step((s - 2) // SLOTS, (s - 2) % SLOTS, lambda d: first[s - d])

        def late_steps(eng, step):
            eng.wait_ge(S["table_d"], 1)
            with eng.Fori(1, (TILES - 3) // SLOTS) as i:
                now = window(eng, tile_exp, i)
                for j in range(SLOTS):
                    step(i, j, lambda d: now[2 + j - d])
            last = window(eng, tile_exp, (TILES - 3) // SLOTS)
            for j in range(3):
                step((TILES - 3) // SLOTS, j, lambda d: last[2 + j - d])

        def lives(i, j, d):
            n = tile_at(i, j, d)[0]
            return not isinstance(n, int) or 0 <= n < TILES

        @block.sync
        def _(sp):
            sp.dma_start(c4[:, :], c_d).then_inc(S["ld_c"], 16)

            def load_xa(u):
                if u >= 2:
                    sp.wait_ge(S["xn1_d"], u - 1)
                sp.dma_start(half(xa, u), half_x(u)).then_inc(ld_xa[u % 2], 16)

            def load_xr(u):
                if u >= 2:
                    sp.wait_ge(S["x1_d"], u - 1)
                sp.dma_start(half(xr, u), half_x(u)).then_inc(ld_xr[u % 2], 16)

            load_xa(0)
            sp.dma_start(wmod[:, :], wmod_d).then_inc(S["ld_wmod"], 16)
            load_xa(1)
            load_xr(0)
            load_xr(1)
            sp.wait_ge(S["consts"], CONSTS)
            sp.dma_start(rows_d[E * REGION:E * REGION + DUMMY * P, :].rearrange("(j p) c -> p j c", p=P),
                         pad_row[:, :].unsqueeze(1).to_broadcast([P, DUMMY, ROW])).then_inc(S["dummy_out"], 16)
            load_xa(2)
            load_xa(3)
            for u in range(2, HALVES):
                if u + 2 < HALVES:
                    load_xa(u + 2)
                load_xr(u)

            def load(i, slot, at):
                if not isinstance(i, int) or i > 0:
                    sp.wait_ge(S["t_fin"], (i - 1) * SLOTS + slot + 1)
                sp.dma_start(tb[slot][:, :], rows_d[bass.ds(at[slot], P), :]).then_inc(loaded[slot], 16)

            sp.wait_ge(S["table0_d"], 1)
            at = window(sp, tile_row, 0)
            for u in range(HALVES // 2):
                sp.wait_ge(rows_out[u % RING], 16 * H)
            for slot in range(SLOTS):
                load(0, slot, at)
            sp.wait_ge(S["pad_at_d"], 1)
            _, pads = nc.values_load_multi_w_load_instructions(
                pad_at[0:1, :], engines=[sp.engine], min_val=0, max_val=E * REGION - P,
                skip_runtime_bounds_check_because="an expert has at most all tokens")
            for e in range(E):
                sp.dma_start(rows_d[bass.ds(pads[e], P), :], pad_row[:, :]).then_inc(S["pads_out"], 16)
            for slot in range(EARLY - SLOTS):
                load(1, slot, at[SLOTS:])
            sp.wait_ge(S["table_d"], 1)
            at = window(sp, tile_row, 1)
            for n, q in enumerate(rows_out):
                sp.wait_ge(q, 16 * H * len(range(n, HALVES, RING)))
            sp.wait_ge(S["pads_out"], 16 * E)
            sp.wait_ge(S["dummy_out"], 16)

            for slot in range(EARLY - SLOTS, SLOTS):
                load(1, slot, at)
            with sp.Fori(2, TILES // SLOTS) as i:
                at = window(sp, tile_row, i)
                for slot in range(SLOTS):
                    load(i, slot, at)
            at = window(sp, tile_row, TILES // SLOTS)
            for slot in range(TILES % SLOTS):
                load(TILES // SLOTS, slot, at)
            for slot in range(SLOTS):
                sp.wait_ge(stored[slot], 16 * ((TILES - 1 - slot) // SLOTS + 1))

        @block.gpsimd
        def _(pool):
            own = [0]

            def chain(ins):
                own[0] += 1
                ins.then_inc(S["pool_own"], 1)
                pool.wait_ge(S["pool_own"], own[0])

            def const(ins):
                ins.then_inc(S["consts"], 1)

            chain(pool.memset(ident[:, :], 0.0))
            const(pool.affine_select(out=ident[:, :], in_=ident[:, :], compare_op=ALU.not_equal, fill=1.0, base=0,
                                     pattern=[[-1, P]], channel_multiplier=1))
            pool.memset(minus_half[:, :], -0.5)
            chain(pool.memset(pick[:, :, :], 0.0))
            const(pool.affine_select(out=pick[:, :, :], in_=pick[:, :, :], compare_op=ALU.not_equal, fill=1.0, base=0,
                                     pattern=[[-1, B], [0, P]], channel_multiplier=1))
            const(pool.memset(ones[:, :], 1.0))
            pool.memset(ident_h[:, :], 0.0)
            pool.memset(mask_h[:, :], 0.0)
            pool.memset(before_h[:, :], 1.0)
            pool.memset(pad_row[:, :], 0.0)
            pool.memset(upto[:, :, :], 1.0)
            pool.memset(ones_h[:, :], 1.0)
            for rows in rows_ring:
                pool.memset(rows[:, :, TOK + 1:ROW], 0.0)
            chain(pool.memset(hot_sum[:, :], 0.0))
            const(pool.affine_select(out=ident_h[:, :], in_=ident_h[:, :], compare_op=ALU.not_equal, fill=1.0, base=0,
                                     pattern=[[-1, P]], channel_multiplier=1))
            const(pool.affine_select(out=mask_h[:, :], in_=mask_h[:, :], compare_op=ALU.is_gt, fill=MASKED, base=0,
                                     pattern=[[-1, P]], channel_multiplier=1))
            const(pool.affine_select(out=before_h[:, :], in_=before_h[:, :], compare_op=ALU.is_gt, fill=0.0, base=0,
                                     pattern=[[1, P]], channel_multiplier=-1))
            const(pool.affine_select(out=upto[:, :, :], in_=upto[:, :, :], compare_op=ALU.is_ge, fill=0.0, base=0,
                                     pattern=[[1, E], [-1, E]], channel_multiplier=0))
            const(pool.memset(pad_row[:, TOK:TOK + 1].bitcast(i32), 1 << 20))
            big = dict(channel_multiplier=0, base=0, allow_small_or_imprecise_dtypes=True)
            const(pool.iota(exp_less8[:, :, :], [[0, NT], [1, E]], **{**big, "base": -E}))
            const(pool.iota(exp_base[:, :, :], [[0, NT], [REGION, E]], **big))
            const(pool.iota(row128[:, :, :], [[0, E], [P, TOKENS // P]], **big))
            const(pool.iota(early_no[:, :], [[1, EARLY]], **big))
            const(pool.iota(tile_no[:, :], [[SLOTS, WINDOWS - 1], [1, WINDOW]], **{**big, "base": SLOTS - EARLY}))
            const(pool.memset(done[:, E:E + 1], 0.0))
            const(pool.iota(tok_no[:, :], [[P, B * NT]], base=0, channel_multiplier=1))

            def pow_half(out, in_, done):
                pool.tensor_tensor(out, in_, minus_half[:, 0:in_.shape[1]], ALU.pow).then_inc(done, 1)

            def rstd1_of(u):
                pool.wait_ge(S["var1_d"], u + 1)
                wait_for(pool, S["xn1_d"], u - 1)
                pow_half(half(rstd1, u), half(var1, u), S["pw1"])

            def rstd2_of(u):
                pool.wait_ge(S["var2_d"], u + 1)
                wait_for(pool, S["xn2_d"], u - 1)
                pow_half(half(rstd2, u), half(var2, u), S["pw2"])

            def shift1(u):
                pool.wait_ge(S["hm1_d"], u + 1)
                wait_for(pool, S["out2_d"], u - 1)
                pool.tensor_tensor(half(h1, u), half(hm1, u), mod(u, SA), ALU.add).then_inc(S["h1_d"], 1)

            def shift2(u):
                pool.wait_ge(S["hm2_d"], u + 1)
                pool.tensor_tensor(rows_ring[u % RING][:, :, H2:H2 + D], half(hm2, u), mod(u, SB), ALU.add).then_inc(S["h2_d"], 1)

            def norm_pow(u):
                pool.wait_ge(S["ssc_d"], u + 1)
                wait_for(pool, S["on_d"], u - 1)
                pow_half(half(rn, u), half(ssc, u), S["pwn"])

            def gated(u):
                pool.wait_ge(S["out2_d"], u + 1)
                mods_of(pool, u)
                wait_for(pool, S["x1_d"], u - 1)
                pool.tensor_tensor(half(og, u), half(out2, u), mod(u, GA), ALU.mult).then_inc(S["og_d"], 1)

            def scatter(u, tiles):
                if 0 in tiles:
                    pool.wait_ge(S["gg_d"], u + 1)
                    pool.wait_ge(S["h2_d"], u + 1)
                    pool.wait_ge(S["pos_d"], group_of(u)[0] + 1)
                for t in tiles:
                    at = group_of(u)[1] + t
                    pool.indirect_dma_start(rows_d[:, :],
                                            bass.IndirectOffsetOnAxis(ap=pos_ring[group_of(u)[0] % 3][:, at:at + 1], axis=0),
                                            rows_ring[u % RING][:, t, :], None).then_inc(rows_out[u % RING], 16)

            rstd1_of(0)
            shift1(0)
            rstd1_of(1)
            pool.wait_ge(S["ema_cl"], 1)
            pow_half(ema[:, 3:4], ema[:, 2:3], S["ema_rn"])
            for m in range(-1, HALVES):
                head = 3 if m + 1 < HALVES else H
                run_at(m - 4, lambda u: scatter(u, range(0, head)))
                if m == HALVES - 1:
                    scatter(m - 3, range(H))
                run_at(m + 1, gated)
                run_at(m + 1, norm_pow)
                run_at(m - 1, shift2)
                run_at(m + 2, shift1)
                run_at(m, rstd2_of)
                run_at(m - 4, lambda u: scatter(u, range(head, H)))
                run_at(m + 3, rstd1_of)
            scatter(HALVES - 3, range(0, 2))
            shift2(HALVES - 1)
            scatter(HALVES - 3, range(2, H))
            for u in range(HALVES - 2, HALVES):
                scatter(u, range(H))

            last_row = pool.snap(TOKENS - 1)

            def put(i, j, _):
                if not lives(i, j, 2):
                    return
                n, slot, rnd = tile_at(i, j, 2)
                pool.wait_ge(S["t_fin"], n + 1)
                pool.sem_inc(S["put_turn"], 1)
                pool.indirect_dma_start(out_rows, bass.IndirectOffsetOnAxis(ap=tok[slot][:, :], axis=0),
                                        ob[slot][:, :], None, bounds_check=last_row, oob_is_err=False)\
                    .then_inc(stored[slot], 16)
            for n in range(SLOTS):
                put(0, n, None)
            with pool.Fori(1, (TILES - 3) // SLOTS) as i:
                for j in range(SLOTS):
                    put(i, j, None)
            for j in range(3):
                put((TILES - 3) // SLOTS, j, None)

        @block.scalar
        def _(act):
            act.dma_start(ema[:, 0:1], ema_d.unsqueeze(1)).then_inc(S["ld_ema"], 16)
            act.wait_ge(S["c_T"], 1)
            act.activation(sil[:, 0, :], banks[:, 7, 0:B], ACT.Exp, scale=-1.0).then_inc(S["c_exp"], 1)
            act.dma_start(scal[:, 0:1], tau_d.unsqueeze(0).to_broadcast([P, 1])).then_inc(S["ld_small"], 16)
            act.dma_start(scal[:, 1:2], blend_d.unsqueeze(0).to_broadcast([P, 1])).then_inc(S["ld_small"], 16)
            act.dma_start(scal[:, 2:3], seq_d.unsqueeze(0).to_broadcast([P, 1])).then_inc(S["ld_small"], 16)
            act.dma_start(rw[:, :], rw_d).then_inc(S["ld_small"], 16)
            act.dma_start(b1_rows[:, :], b1_d.rearrange("e (c p) -> (e c) p", p=P)).then_inc(S["ld_b1"], 16)
            act.dma_start(rb[:, :], rb_d.unsqueeze(0).to_broadcast([P, E])).then_inc(S["ld_small"], 16)
            def normed(u, src, out, rstd, nbias, done):
                for t in range(H):
                    at = H * (u % 2) + t
                    ins = act.activation(out[:, at, :], src(t), ACT.Identity, bias=nbias[:, at:at + 1], scale=rstd[:, at:at + 1])
                ins.then_inc(done, 1)

            def normed1(u):
                act.wait_ge(S["nb1"], u + 1)
                wait_for(act, S["hm1_d"], u - 1)
                normed(u, lambda t: xa[:, H * (u % 2) + t, :], xn1, rstd1, nbias1, S["xn1_d"])

            def normed2(u):
                act.wait_ge(S["nb2"], u + 1)
                wait_for(act, S["hm2_d"], u - 1)
                normed(u, lambda t: rows_ring[u % RING][:, t, X1:X1 + D], xn2, rstd2, nbias2, S["xn2_d"])

            def mods_out(b, part):
                first, last = MOD_PARTS[part]
                act.wait_ge(S["mod_ps"], 2 * b + part + 1)
                act.activation(mods[:, b, first:last, :].rearrange("p a d -> p (a d)"),
                               p_sim[(b + 1) % 2][:, 512 * part:512 * part + (last - first) * D], ACT.Copy).then_inc(S["mod_sb"], 1)

            def square(u):
                act.wait_ge(S["h1_d"], u + 1)
                wait_for(act, S["wg_d"], u - 1)
                act.activation(half(sq, u), half(h1, u), ACT.Square).then_inc(S["sq_d"], 1)

            def tanh(u):
                act.wait_ge(S["wg_d"], u + 1)
                wait_for(act, S["out2_d"], u - 1)
                act.activation(half(th, u), half(wg, u), ACT.Tanh, scale=GELU_C * GELU_A).then_inc(S["th_d"], 1)

            def norms(u):
                act.wait_ge(S["out2_d"], u + 1)
                wait_for(act, S["ssc_d"], u - 1)
                for t in range(H):
                    at = H * (u % 2) + t
                    ins = act.activation(junk[:, at, :], out2[:, at, :], ACT.Square, accum_out=ss[:, at:at + 1])
                ins.then_inc(S["ss_d"], 1)

            def novelty(u):
                act.wait_ge(S["fam_d"], u + 1)
                act.activation(half(nov, u), half(fam, u), ACT.Exp, scale=scal2[:, 4:5]).then_inc(S["nov_d"], 1)
                act.wait_ge(S["nov_d"], u + 1)
                wait_for(act, S["x1_d"], u - 1)
                act.activation(half(gate, u), half(nov, u), ACT.Identity, scale=scal2[:, 5:6], bias=scal[:, 1:2])\
                   .then_inc(S["gate_d"], 1)

            def unit(u):
                act.wait_ge(S["pwn"], u + 1)
                wait_for(act, S["tr1"], u - 1)
                for t in range(H):
                    at = H * (u % 2) + t
                    ins = act.activation(on[:, at, :], out2[:, at, :], ACT.Copy, scale=rn[:, at:at + 1])
                ins.then_inc(S["on_d"], 1)

            def onT_out(u):
                act.wait_ge(S["tr1"], u + 1)
                wait_for(act, S["ema_d2"], 2 * (u // 2) - 2)
                a = T // 2 * (u % 2)
                act.activation(onT2[u // 2 % 2][:, a:a + T // 2], p_on, ACT.Copy).then_inc(S["onT_d"], 1)

            def h2T_out(u):
                act.wait_ge(S["tr2"], u + 1)
                if u >= 2:
                    act.wait_ge(S["rt_d"], group_of(u - 2)[0] + 1)
                a = T // 2 * (u % 2)
                act.activation(h2T[:, a:a + T // 2], p_h2, ACT.Copy).then_inc(S["h2T_d"], 1)

            def router_exp(g):
                act.wait_ge(S["lz_d"], g + 1)
                n = tiles_of(g)
                act.activation(lexp[:, 0:n, :], lz[:, 0:n, :], ACT.Exp).then_inc(S["lexp_d"], 1)

            def row_gates(u):
                g, first = group_of(u)
                act.wait_ge(S["top_d"], g + 1)
                mods_of(act, u)
                src = mods[:, u // 2, GB, :]
                rows = rows_ring[u % RING]
                wait_for(act, rows_out[u % RING], 16 * H * (u // RING))
                for t in range(H):
                    act.activation(rows[:, t, GG:GG + D], src, ACT.Copy, scale=top[:, first + t:first + t + 1])
                toks = tok_no[:, u * H:u * H + H]
                act.activation(rows[:, :, TOK:TOK + 1].bitcast(i32).squeeze(2), toks, ACT.Copy).then_inc(S["gg_d"], 1)

            def tile_step(i, j, expert):
                if lives(i, j, 0):
                    n, slot, _ = tile_at(i, j, 0)
                    wait_for(act, S["t_hid"], n - 1)
                    act.activation(w1s[slot % 2][:, :], w1[:, bass.ds(expert(0) * F, F)], ACT.Copy).then_inc(S["t_w1s"], 1)
                    act.wait_ge(S["t_h2T"], n + 1)
                    act.activation(h2s[slot % 2][:, :], p_h2T[slot % 2], ACT.Copy).then_inc(S["t_h2s"], 1)
                if lives(i, j, 1):
                    n, slot, _ = tile_at(i, j, 1)
                    act.wait_ge(S["t_hidb"], n + 1)
                    wait_for(act, S["t_y"], n - 1)
                    act.activation(hid[slot % 2][:, :], hidb[slot % 2][:, :], ACT.Relu).then_inc(S["t_hidr"], 1)
            normed1(0)
            mods_out(0, 0)
            square(0)
            mods_out(0, 1)
            act.wait_ge(S["ld_small"], 80)
            act.activation(scal2[:, 0:1], scal[:, 0:1], ACT.Exp).then_inc(S["scal_e"], 1)
            act.activation(scal2[:, 1:3], scal[:, 1:3], ACT.Exp, scale=-1.0).then_inc(S["scal_e"], 1)
            act.dma_start(w1[:, :].rearrange("p (e f) -> p e f", e=E), w1_d.rearrange("e d f -> d e f")).then_inc(S["ld_w1"], 16)
            act.dma_start(w2[:, :].rearrange("p (e c d) -> p e c d", e=E, c=FC),
                          w2_d.rearrange("e (c p) d -> p e c d", p=P)).then_inc(S["ld_w2"], 16)
            act.dma_start(b2[:, :], b2_d.rearrange("e d -> (e d)").unsqueeze(0).to_broadcast([P, E * D])).then_inc(S["ld_b"], 16)
            for m in range(-1, HALVES):
                if m == HALVES - 1:
                    row_gates(m - 3)
                run_at(m - 1, normed2)
                run_at(m + 1, tanh)
                if m == -1:
                    mods_out(1, 0)
                    mods_out(1, 1)
                if m == -1:
                    norms(0)
                run_at(m + 2, normed1)
                if m == -1:
                    mods_out(2, 0)
                    mods_out(2, 1)
                else:
                    run_at(m + 1, norms)
                run_at(m, novelty)
                if m == -1:
                    mods_out(3, 0)
                    mods_out(3, 1)
                    act.wait_ge(S["scal_ok"], 1)
                if m == 0:
                    act.wait_ge(S["b1_T"], 1)
                    act.activation(b1[:, :], p_b1, ACT.Copy).then_inc(S["b1_ok"], 1)
                run_at(m + 1, unit)
                run_at(m + 1, onT_out)
                run_at(m + 2, square)
                if m == HALVES - 1:
                    act.wait_ge(S["ld_w1"], 16)
                    early = early_steps(act, tile_step)
                    early(0)
                run_at(m - 1, h2T_out)
                if m % 2 == 0:
                    run_at(m - 3, row_gates)
                router_at(m, router_exp)
                if m % 2 == 1 and m < HALVES - 1:
                    run_at(m - 3, row_gates)
            row_gates(HALVES - 3)
            normed2(HALVES - 1)
            early(1)
            router_exp(len(GROUPS) - 2)
            row_gates(HALVES - 2)
            h2T_out(HALVES - 1)
            router_exp(len(GROUPS) - 1)
            row_gates(HALVES - 1)
            for n in range(2, EARLY):
                early(n)
            late_steps(act, tile_step)

        @block.vector
        def _(dve):
            prep = [0]

            def chain(ins):
                prep[0] += 1
                ins.then_inc(S["dve_prep"], 1)
                dve.wait_ge(S["dve_prep"], prep[0])

            def stats(u, src, st, mv, var, done_bn, done_mv, done_var, used):
                for t in range(H):
                    ins = dve.bn_stats(st[:, H * (u % 2) + t, :], src(t))
                ins.then_inc(done_bn, 1)
                dve.wait_ge(done_bn, u + 1)
                wait_for(dve, used, u - 1)
                for t in range(H):
                    at = H * (u % 2) + t
                    ins = dve.bn_aggr(mv[:, at, :], st[:, at, :])
                ins.then_inc(done_mv, 1)
                dve.wait_ge(done_mv, u + 1)
                dve.tensor_scalar(half(var, u), half(mv, u)[:, :, 1], LN_EPS, None, ALU.add).then_inc(done_var, 1)

            def stats1(u):
                dve.wait_ge(ld_xa[u % 2], 16 * (u // 2) + 16)
                wait_for(dve, S["pw1"], u - 1)
                stats(u, lambda t: xa[:, H * (u % 2) + t, :], st1, mv1, var1, S["bn1"], S["mv1_d"], S["var1_d"], S["nb1"])

            def bias1(u):
                dve.wait_ge(S["pw1"], u + 1)
                wait_for(dve, S["xn1_d"], u - 1)
                dve.scalar_tensor_tensor(half(nbias1, u), half(mv1, u)[:, :, 0], -1.0, half(rstd1, u), ALU.mult, ALU.mult)\
                   .then_inc(S["nb1"], 1)

            def scale1(u):
                dve.wait_ge(S["xn1_d"], u + 1)
                dve.wait_ge(S["mod_sb"], 2 * (u // 2) + 1)
                wait_for(dve, S["h1_d"], u - 1)
                dve.tensor_tensor(half(hm1, u), half(xn1, u), mod(u, CA), ALU.mult).then_inc(S["hm1_d"], 1)

            def gelu_in(u):
                dve.wait_ge(S["sq_d"], u + 1)
                wait_for(dve, S["th_d"], u - 1)
                dve.scalar_tensor_tensor(half(wg, u), half(sq, u), 1.0 / GELU_A, half(h1, u), ALU.add, ALU.mult)\
                   .then_inc(S["wg_d"], 1)

            def gelu_out(u):
                dve.wait_ge(S["th_d"], u + 1)
                wait_for(dve, S["og_d"], u - 1)
                wait_for(dve, S["on_d"], u - 1)
                dve.scalar_tensor_tensor(half(out2, u), half(th, u), 1.0, half(h1, u), ALU.add, ALU.mult)\
                   .then_inc(S["out2_d"], 1)

            def norm_clamp(u):
                dve.wait_ge(S["ss_d"], u + 1)
                wait_for(dve, S["pwn"], u - 1)
                dve.tensor_scalar(half(ssc, u), half(ss, u), 4e-24, None, ALU.max).then_inc(S["ssc_d"], 1)

            def nearest(u, t):
                dve.wait_ge(S["sim_d"], H * u + t + 1)
                at = H * (u % 2) + t
                if t == 0:
                    wait_for(dve, S["fam_d"], u - 1)
                dve.tensor_reduce(mx[:, at:at + 1], p_sim[t % 2][:, 0:(at + 1) * P], AX.X, ALU.max).then_inc(S["mx_d"], 1)

            def familiarity(u):
                dve.wait_ge(S["ema_d2"], u + 1)
                dve.wait_ge(S["mx_d"], H * u + H)
                if u % 2 == 0:
                    dve.tensor_copy(mx[0:1, 0:1], p_ema[0:1, 0, 0:1]).then_inc(S["mx0_d"], 1)
                    dve.wait_ge(S["mx0_d"], u // 2 + 1)
                wait_for(dve, S["nov_d"], u - 1)
                dve.scalar_tensor_tensor(half(fam, u), half(mx, u), w_seq, p_ema[:, :, 1], ALU.mult, ALU.add).then_inc(S["fam_d"], 1)

            def residual(u):
                rows = rows_ring[u % RING]
                dve.wait_ge(S["gate_d"], u + 1)
                dve.wait_ge(S["og_d"], u + 1)
                dve.wait_ge(ld_xr[u % 2], 16 * (u // 2) + 16)
                wait_for(dve, rows_out[u % RING], 16 * H * (u // RING))
                for t in range(H):
                    at = H * (u % 2) + t
                    ins = dve.scalar_tensor_tensor(rows[:, t, X1:X1 + D], og[:, at, :], gate[:, at:at + 1], xr[:, at, :],
                                                   ALU.mult, ALU.add)
                ins.then_inc(S["x1_d"], 1)

            def stats2(u):
                dve.wait_ge(S["x1_d"], u + 1)
                wait_for(dve, S["pw2"], u - 1)
                stats(u, lambda t: rows_ring[u % RING][:, t, X1:X1 + D], st2, mv2, var2,
                      S["bn2"], S["mv2_d"], S["var2_d"], S["nb2"])

            def bias2(u):
                dve.wait_ge(S["pw2"], u + 1)
                wait_for(dve, S["xn2_d"], u - 1)
                dve.scalar_tensor_tensor(half(nbias2, u), half(mv2, u)[:, :, 0], -1.0, half(rstd2, u), ALU.mult, ALU.mult)\
                   .then_inc(S["nb2"], 1)

            def scale2(u):
                dve.wait_ge(S["xn2_d"], u + 1)
                dve.wait_ge(S["mod_sb"], 2 * (u // 2) + 2)
                wait_for(dve, S["h2_d"], u - 1)
                dve.tensor_tensor(half(hm2, u), half(xn2, u), mod(u, CB), ALU.mult).then_inc(S["hm2_d"], 1)

            def router_a(g):
                n = tiles_of(g)
                dve.wait_ge(S["rt_d"], g + 1)
                dve.tensor_tensor(lg[:, 0:n, :], p_logit[:, 0:n, :], rb[:, :].unsqueeze(1).to_broadcast([P, n, E]), ALU.add)\
                   .then_inc(S["lg_d"], 1)
                dve.wait_ge(S["lg_d"], g + 1)
                dve.tensor_reduce(lmax[:, 0:n], lg[:, 0:n, :], AX.X, ALU.max).then_inc(S["lmax_d"], 1)
                dve.wait_ge(S["lmax_d"], g + 1)
                dve.tensor_tensor(lz[:, 0:n, :], lg[:, 0:n, :], of_value(lmax[:, 0:n], E), ALU.subtract).then_inc(S["lz_d"], 1)
                dve.wait_ge(S["lz_d"], g + 1)
                dve.scalar_tensor_tensor(cand[:, 0:n, :], lz[:, 0:n, :], 0.0, exp_less8[:, 0:n, :], ALU.is_equal, ALU.mult)\
                   .then_inc(S["cand_d"], 1)
                dve.wait_ge(S["cand_d"], g + 1)
                dve.tensor_reduce(cmin[:, 0:n], cand[:, 0:n, :], AX.X, ALU.min).then_inc(S["cmin_d"], 1)
                dve.wait_ge(S["cmin_d"], g + 1)
                dve.tensor_tensor(hot[:, 0:n, :], exp_less8[:, 0:n, :], of_value(cmin[:, 0:n], E), ALU.is_equal).then_inc(S["hot_d"], 1)

            def router_b(g):
                n = tiles_of(g)
                dve.wait_ge(S["lexp_d"], g + 1)
                dve.tensor_reduce(lsum[:, 0:n], lexp[:, 0:n, :], AX.X, ALU.add).then_inc(S["lsum_d"], 1)
                dve.wait_ge(S["lsum_d"], g + 1)
                wait_for(dve, S["gg_d"], GROUPS[g][0][0])
                dve.reciprocal(top[:, 0:n], lsum[:, 0:n]).then_inc(S["top_d"], 1)

            def place(g):
                n = tiles_of(g)
                dve.wait_ge(S["rank_d"], g + 1)
                dve.tensor_tensor(placed[:, 0:n, :], p_rank[:, 0:n, :], exp_base[:, 0:n, :], ALU.add).then_inc(S["pl_d"], 1)
                dve.tensor_reduce(hot_new[:, :], hot[:, 0:n, :].rearrange("p t e -> p e t"), AX.X, ALU.add).then_inc(S["hotn_d"], 1)
                dve.wait_ge(S["pl_d"], g + 1)
                dve.tensor_tensor(placed2[:, 0:n, :], placed[:, 0:n, :], hot[:, 0:n, :], ALU.mult).then_inc(S["pl2_d"], 1)
                dve.wait_ge(S["hotn_d"], g + 1)
                dve.tensor_tensor(hot_sum[:, :], hot_sum[:, :], hot_new[:, :], ALU.add).then_inc(S["hots_d"], 1)
                dve.wait_ge(S["pl2_d"], g + 1)
                dve.tensor_reduce(posf[:, 0:n], placed2[:, 0:n, :], AX.X, ALU.add).then_inc(S["posf_d"], 1)
                dve.wait_ge(S["posf_d"], g + 1)
                if g >= 3:
                    for u in GROUPS[g - 3][0]:
                        dve.wait_ge(rows_out[u % RING], 16 * H * (u // RING + 1))
                dve.tensor_copy(pos_ring[g % 3][:, 0:n], posf[:, 0:n]).then_inc(S["pos_d"], 1)

            dve.wait_ge(S["c_exp"], 1)
            chain(dve.tensor_scalar(sil[:, 1, :], sil[:, 0, :], 1.0, None, ALU.add))
            chain(dve.reciprocal(sil[:, 2, :], sil[:, 1, :]))
            dve.tensor_tensor(sil[:, 3, :], sil[:, 2, :], banks[:, 7, 0:B], ALU.mult).then_inc(S["c_sil"], 1)
            stats1(0)

            dve.wait_ge(S["mod_raw"], 1)
            raw = p_mod4.rearrange("b (a d) -> b a d", a=6)
            dve.tensor_copy(mod4[:, SA::3, :], raw[:, SA::3, :])
            dve.tensor_scalar(mod4[:, CA::3, :], raw[:, CA::3, :], 1.0, None, ALU.add).then_inc(S["mod4_ok"], 1)
            bias1(0)
            chain(dve.tensor_copy(mod4[:, GA::3, :], raw[:, GA::3, :]))
            g = mod4[:, GA::3, :]
            dve.tensor_scalar(gsign[:, :, :], g, 0.0, 2.0, ALU.is_ge, ALU.mult)
            chain(dve.scalar_tensor_tensor(gabs[:, :, :], g, -1.0, g, ALU.mult, ALU.max))
            dve.tensor_scalar(gmag[:, 0, :], gabs[:, 0, :], 0.25, 0.5, ALU.max, ALU.mult)
            chain(dve.tensor_scalar(gmag[:, 1, :], gabs[:, 1, :], 0.25, None, ALU.max))
            dve.scalar_tensor_tensor(g, gsign[:, :, :], -1.0, gmag[:, :, :], ALU.add, ALU.mult).then_inc(S["mod4_ok"], 1)
            dve.wait_ge(S["ld_ema"], 16)
            dve.tensor_tensor(ema[:, 1:2], ema[:, 0:1], ema[:, 0:1], ALU.mult).then_inc(S["ema_sq"], 1)
            scale1(0)
            stats1(1)
            dve.wait_ge(S["ema_ss"], 1)
            dve.tensor_scalar(ema[:, 2:3], banks[:, 6, 0:1], 1e-24, None, ALU.max).then_inc(S["ema_cl"], 1)
            dve.wait_ge(S["scal_e"], 2)
            chain(dve.tensor_scalar(scal2[:, 4:5], scal2[:, 0:1], -1.0, None, ALU.mult))
            chain(dve.tensor_scalar(scal[:, 1:3], scal2[:, 1:3], 1.0, None, ALU.add))
            chain(dve.reciprocal(scal2[:, 5:7], scal[:, 1:3]))
            dve.tensor_scalar(scal[:, 1:3], scal2[:, 5:7], -1.0, 1.0, ALU.mult, ALU.add).then_inc(S["scal_ok"], 1)
            dve.wait_ge(S["ema_rn"], 1)
            dve.tensor_tensor(ema_n[:, 0:1], ema[:, 0:1], ema[:, 3:4], ALU.mult).then_inc(S["ema_n"], 1)
            dve.wait_ge(S["ema_n"], 1)
            dve.wait_ge(S["scal_ok"], 1)
            dve.tensor_tensor(ema_n[:, 1:2], ema_n[:, 0:1], scal[:, 2:3], ALU.mult).then_inc(S["ema_n"], 1)
            w_seq = scal2[:, 6:7]
            dve.wait_ge(S["scal_ok"], 1)
            dve.wait_ge(S["consts"], CONSTS)
            chain(dve.tensor_scalar(tile_no[:, :], tile_no[:, :], float(TILES - 1 - EARLY), None, ALU.min))

            def tile_step(i, j, expert):
                if lives(i, j, 1):
                    n, slot, _ = tile_at(i, j, 1)
                    dve.wait_ge(S["t_hid"], n + 1)
                    wait_for(dve, S["t_hidr"], n - 1)
                    bias = b1[:, bass.ds(expert(1) * FC, FC)].unsqueeze(2).to_broadcast([P, FC, P])
                    dve.tensor_tensor(hidb[slot % 2][:, :].rearrange("p (c n) -> p c n", c=FC),
                                      p_hid[slot % 2].rearrange("p (c n) -> p c n", c=FC), bias, ALU.add)\
                       .then_inc(S["t_hidb"], 1)
                if lives(i, j, 2):
                    n, slot, rnd = tile_at(i, j, 2)
                    dve.wait_ge(S["t_y"], n + 1)
                    dve.tensor_tensor(y1[:, :], p_y[slot % 2], b2[:, bass.ds(expert(2) * D, D)], ALU.add).then_inc(S["t_y1"], 1)
                    wait_for(dve, stored[slot], rnd * 16)
                    dve.tensor_copy(tok[slot][:, :], tb[slot][:, TOK:TOK + 1].bitcast(i32))
                    dve.wait_ge(S["t_y1"], n + 1)
                    dve.tensor_tensor(y2[:, :], y1[:, :], tb[slot][:, GG:GG + D], ALU.mult).then_inc(S["t_y2"], 1)
                    dve.wait_ge(S["t_y2"], n + 1)
                    dve.tensor_tensor(ob[slot][:, :], y2[:, :], tb[slot][:, X1:X1 + D], ALU.add).then_inc(S["t_fin"], 1)
            own0 = [0]

            def tab0(ins):
                own0[0] += 1
                ins.then_inc(S["tab0_own"], 1)
                dve.wait_ge(S["tab0_own"], own0[0])

            def early_table_a():
                dve.wait_ge(S["cnt0_ok"], 1)
                tab0(dve.tensor_tensor(cmp0[:, :, :], cnt0[:, :].unsqueeze(2).to_broadcast([1, E, TOKENS // 2 // P]),
                                       row128[:, :, 1:TOKENS // 2 // P + 1], ALU.is_ge))
                dve.tensor_reduce(full[:, :], cmp0[:, :, :], AX.X, ALU.add).then_inc(S["tab0_own"], 1)

            def early_table_b():
                dve.wait_ge(S["tab0_own"], 2)
                own0[0] = 2
                tab0(dve.tensor_tensor(cum0[:, :, :], upto[:, :, :], full[:, :].unsqueeze(1).to_broadcast([1, E, E]), ALU.mult))
                dve.tensor_reduce(fend[:, :], cum0[:, :, :], AX.X, ALU.add).then_inc(S["tab0_own"], 1)

            def early_table_c():
                dve.wait_ge(S["tab0_own"], 4)
                dve.tensor_tensor(room[:, :], fend[:, :], full[:, :], ALU.subtract)
                dve.tensor_tensor(past0[:, :, :], early_no[:, :].unsqueeze(2).to_broadcast([1, EARLY, E]),
                                  fend[:, :].unsqueeze(1).to_broadcast([1, EARLY, E]), ALU.is_ge).then_inc(S["tab0_own"], 1)

            def early_table_d():
                dve.wait_ge(S["tab0_own"], 5)
                dve.tensor_scalar(room2[:, :], room[:, :], -1.0, float(EARLY), ALU.mult, ALU.add)
                dve.tensor_reduce(ek0[:, :], past0[:, :, :], AX.X, ALU.add)
                own0[0] = 5
                tab0(dve.tensor_tensor(past0_n[:, :, :], past0[:, :, :], full[:, :].unsqueeze(1).to_broadcast([1, EARLY, E]), ALU.mult))
                dve.scalar_tensor_tensor(done[:, 0:E], room2[:, :], 0.0, full[:, :], ALU.max, ALU.min)
                dve.tensor_scalar(tile_exp[:, 0:EARLY], ek0[:, :], float(E - 1), None, ALU.min)
                dve.tensor_reduce(skipped0[:, :], past0_n[:, :, :], AX.X, ALU.add).then_inc(S["tab0_own"], 1)

            def early_table_e():
                dve.wait_ge(S["tab0_own"], 7)
                own0[0] = 7
                tab0(dve.tensor_tensor(rk0[:, :], early_no[:, :], skipped0[:, :], ALU.subtract))
                tab0(dve.tensor_scalar(rk02[:, :], rk0[:, :], float(P), None, ALU.mult))
                dve.scalar_tensor_tensor(tile_row[:, 0:EARLY], ek0[:, :], float(REGION), rk02[:, :], ALU.mult, ALU.add)\
                   .then_inc(S["table0_d"], 1)

            for m in range(-1, HALVES):
                run_at(m, lambda u: nearest(u, 0))
                if m == HALVES - 1:
                    early_table_a()
                router_at(m - 1, place)
                run_at(m - 1, bias2)
                run_at(m + 2, bias1)
                if m == HALVES - 1:
                    early_table_b()
                run_at(m, lambda u: nearest(u, 1))
                if m == HALVES - 1:
                    early_table_c()
                run_at(m + 1, gelu_in)
                run_at(m, lambda u: nearest(u, 2))
                if m == HALVES - 1:
                    early_table_d()
                run_at(m + 1, gelu_out)
                run_at(m, lambda u: nearest(u, 3))
                if m == HALVES - 1:
                    early_table_e()
                if m == HALVES - 2:
                    dve.wait_ge(S["cnt0_d"], 1)
                    dve.tensor_copy(cnt0[:, :], p_count[0:1, :]).then_inc(S["cnt0_ok"], 1)
                run_at(m, familiarity)
                run_at(m + 1, norm_clamp)
                run_at(m - 1, scale2)
                run_at(m, residual)
                run_at(m + 2, scale1)
                router_at(m, router_a)
                run_at(m, stats2)
                run_at(m + 3, stats1)
                router_at(m, router_b)
            dve.wait_ge(S["ld_b"], 16)
            dve.wait_ge(S["b1_ok"], 1)
            early = early_steps(dve, tile_step)
            early(0)
            router_at(HALVES - 1, place)
            own = [0]

            def tab(ins):
                own[0] += 1
                ins.then_inc(S["tab_own"], 1)
                dve.wait_ge(S["tab_own"], own[0])

            def table_a():
                dve.wait_ge(S["cnt_d"], 1)
                tab(dve.tensor_copy(cnt[:, :], p_count[0:1, :]))
                dve.tensor_tensor(pad_at[:, :], cnt[:, :], exp_base[0:1, 0, :], ALU.add).then_inc(S["pad_at_d"], 1)
                tab(dve.tensor_tensor(cmp1[:, :, :], cnt[:, :].unsqueeze(2).to_broadcast([1, E, TOKENS // P]), row128[:, :, 0:TOKENS // P], ALU.is_gt))
                tab(dve.tensor_reduce(ntile[:, :], cmp1[:, :, :], AX.X, ALU.add))
                dve.tensor_tensor(beside[:, :], ntile[:, :], done[:, 1:E + 1], ALU.subtract)
                tab(dve.tensor_tensor(left[:, :], ntile[:, :], done[:, 0:E], ALU.subtract))
                tab(dve.tensor_tensor(cum[:, :, :], upto[:, :, :], left[:, :].unsqueeze(1).to_broadcast([1, E, E]), ALU.mult))
                tab(dve.tensor_reduce(tend[:, :], cum[:, :, :], AX.X, ALU.add))

            def table_b():
                tab(dve.tensor_tensor(past[:, :, :], tile_no[:, :].unsqueeze(2).to_broadcast([1, LATE, E]),
                                      tend[:, :].unsqueeze(1).to_broadcast([1, LATE, E]), ALU.is_ge))
                tab(dve.tensor_reduce(ek[:, :], past[:, :, :], AX.X, ALU.add))
                tab(dve.tensor_tensor(past_n[:, :, :], past[:, :, :], beside[:, :].unsqueeze(1).to_broadcast([1, LATE, E]), ALU.mult))
                tab(dve.tensor_reduce(skipped[:, :], past_n[:, :, :], AX.X, ALU.add))
                tab(dve.scalar_tensor_tensor(rk[:, :], tile_no[:, :], done[:, 0:1], skipped[:, :], ALU.add, ALU.subtract))
                tab(dve.tensor_scalar(rk2[:, :], rk[:, :], float(P), None, ALU.mult))
                tab(dve.scalar_tensor_tensor(tile_row[:, WINDOW:], ek[:, :], float(REGION), rk2[:, :], ALU.mult, ALU.add))
                tab(dve.tensor_scalar(tile_exp[:, WINDOW:], ek[:, :], float(E - 1), None, ALU.min))
                dve.tensor_copy(tile_exp[:, WINDOW:WINDOW + EARLY - SLOTS], tile_exp[:, SLOTS:EARLY])
                dve.tensor_copy(tile_row[:, WINDOW:WINDOW + EARLY - SLOTS], tile_row[:, SLOTS:EARLY]).then_inc(S["table_d"], 1)

            bias2(HALVES - 1)
            early(1)
            router_a(len(GROUPS) - 2)
            scale2(HALVES - 1)
            router_b(len(GROUPS) - 2)
            place(len(GROUPS) - 2)
            router_a(len(GROUPS) - 1)
            router_b(len(GROUPS) - 1)
            place(len(GROUPS) - 1)
            table_a()
            table_b()
            for n in range(2, EARLY):
                early(n)
            late_steps(dve, tile_step)

        @block.tensor
        def _(pe):
            pe.wait_ge(S["consts"], 1)
            pe.wait_ge(S["ld_c"], 16)
            pe.transpose(banks[:, 7, 0:B], c4[:, :], ident[0:B, 0:B]).then_inc(S["c_T"], 1)
            pe.wait_ge(S["c_sil"], 1)
            pe.wait_ge(S["ld_wmod"], 16)
            pe.matmul(p_mod4[:, 0:512], sil[:, 3, :], wmod[:, 0:512], start=True, stop=True)
            pe.matmul(p_mod4[:, 512:6 * D], sil[:, 3, :], wmod[:, 512:6 * D], start=True, stop=True).then_inc(S["mod_raw"], 1)

            def spread(b, part):
                first, last = MOD_PARTS[part]
                pe.matmul(p_sim[(b + 1) % 2][:, 512 * part:512 * part + (last - first) * D], pick[:, b, :],
                          mod4[:, first:last, :].rearrange("b a d -> b (a d)"), start=True, stop=True).then_inc(S["mod_ps"], 1)

            pe.wait_ge(S["consts"], 3)
            pe.wait_ge(S["mod4_ok"], 1)
            spread(0, 0)
            pe.wait_ge(S["mod4_ok"], 2)
            spread(0, 1)
            pe.wait_ge(S["ema_sq"], 1)
            pe.matmul(banks[:, 6, 0:1], ones[:, :], ema[:, 1:2], start=True, stop=True).then_inc(S["ema_ss"], 1)
            for b in range(1, B):
                for part in range(2):
                    if b >= 2:
                        pe.wait_ge(S["mod_sb"], 2 * (b - 2) + part + 1)
                    spread(b, part)
            pe.wait_ge(S["ld_b1"], 16)
            pe.transpose(p_b1, b1_rows[:, :], ident[0:E * FC, 0:E * FC]).then_inc(S["b1_T"], 1)
            pe.wait_ge(S["consts"], 6)
            pe.wait_ge(S["ema_n"], 2)
            pe.wait_ge(S["ld_small"], 80)

            def keep_warm(n):
                for _ in range(n):
                    pe.matmul(p_on, ones_h[:, :], ones_h[:, :].unsqueeze(1).to_broadcast([P, H, P]), start=True, stop=True)

            def turn_on(u):
                pe.wait_ge(S["on_d"], u + 1)
                wait_for(pe, S["onT_d"], u)
                for t in range(H):
                    ins = pe.transpose(p_on[:, t * P:(t + 1) * P], on[:, H * (u % 2) + t, :], ident[:, :])
                ins.then_inc(S["tr1"], 1)

            def turn_h2(u):
                pe.wait_ge(S["h2_d"], u + 1)
                wait_for(pe, S["h2T_d"], u)
                for t in range(H):
                    ins = pe.transpose(p_h2[:, t * P:(t + 1) * P], rows_ring[u % RING][:, t, H2:H2 + D], ident[:, :])
                ins.then_inc(S["tr2"], 1)

            def sims(u):
                onT = onT2[u // 2 % 2]
                for t in range(H):
                    wait_for(pe, S["mx_d"], H * u + t - 1)
                    if t == 0:
                        pe.wait_ge(S["onT_d"], u + 1)
                        if u == 0:
                            pe.wait_ge(S["mod_sb"], 2 * B)
                    at = H * (u % 2) + t
                    mine = onT[:, at * P:(at + 1) * P]
                    n = (at + 1) * P
                    for c in range(0, n, 512):
                        w = min(512, n - c)
                        last = c + w == n
                        ins = pe.matmul(p_sim[t % 2][:, c:c + w], mine, onT[:, c:c + w], start=True, stop=not last)
                        if last:
                            ins = pe.matmul(p_sim[t % 2][:, n - P:n], ident_h[:, :], mask_h[:, :], start=False, stop=True)
                    ins.then_inc(S["sim_d"], 1)

            def ema_sims(u):
                wait_for(pe, S["fam_d"], u)
                a = T // 2 * (u % 2)
                for t in range(H):
                    ins = pe.matmul(p_ema[:, t, :], onT2[u // 2 % 2][:, a + t * P:a + (t + 1) * P], ema_n[:, :],
                                    start=True, stop=True)
                ins.then_inc(S["ema_d2"], 1)

            def router(g):
                wait_for(pe, S["pl_d"], g)
                if g == 0:
                    pe.wait_ge(S["b1_ok"], 1)
                if g == 2:
                    pe.wait_ge(S["cnt0_ok"], 1)
                for n, u in enumerate(GROUPS[g][0]):
                    pe.wait_ge(S["h2T_d"], u + 1)
                    for t in range(H):
                        at = H * (u % 2) + t
                        ins = pe.matmul(p_logit[:, H * n + t, :], h2T[:, at * P:(at + 1) * P], rw[:, :], start=True, stop=True)
                ins.then_inc(S["rt_d"], 1)

            def rank(g):
                pe.wait_ge(S["hot_d"], g + 1)
                wait_for(pe, S["hots_d"], g)
                n = tiles_of(g)
                pe.matmul(p_rank[:, 0:n, :], before_h[:, :], hot[:, 0:n, :], start=True, stop=False)
                for t in range(n - 1):
                    pe.matmul(p_rank[:, t + 1:n, :], ones_h[:, :], hot[:, t:t + 1, :].to_broadcast([P, n - 1 - t, E]),
                              start=False, stop=False)
                pe.matmul(p_rank[:, 0:n, :], ones_h[:, :], hot_sum[:, :].unsqueeze(1).to_broadcast([P, n, E]),
                          start=False, stop=True).then_inc(S["rank_d"], 1)

            def tile_step(i, j, expert):
                if lives(i, j, 0):
                    n, slot, rnd = tile_at(i, j, 0)
                    pe.wait_ge(loaded[slot], (rnd + 1) * 16)
                    wait_for(pe, S["t_h2s"], n - 1)
                    pe.transpose(p_h2T[slot % 2], tb[slot][:, H2:H2 + D], ident[:, :]).then_inc(S["t_h2T"], 1)
                if lives(i, j, 1):
                    n, slot, _ = tile_at(i, j, 1)
                    pe.wait_ge(S["t_w1s"], n + 1)
                    pe.wait_ge(S["t_h2s"], n + 1)
                    wait_for(pe, S["t_hidb"], n - 1)
                    for c in range(FC):
                        ins = pe.matmul(p_hid[slot % 2][:, c * P:(c + 1) * P], w1s[slot % 2][:, c * P:(c + 1) * P],
                                        h2s[slot % 2][:, :], start=True, stop=True)
                    ins.then_inc(S["t_hid"], 1)
                if lives(i, j, 2):
                    n, slot, _ = tile_at(i, j, 2)
                    pe.wait_ge(S["t_hidr"], n + 1)
                    wait_for(pe, S["t_y1"], n - 1)
                    for c in range(FC):
                        ins = pe.matmul(p_y[slot % 2], hid[slot % 2][:, c * P:(c + 1) * P],
                                        w2[:, bass.ds(expert(2) * (FC * D) + c * D, D)], start=(c == 0), stop=(c == FC - 1))
                    ins.then_inc(S["t_y"], 1)
            for m in range(-1, HALVES):
                run_at(m, sims)
                if m == HALVES - 2:
                    pe.wait_ge(S["pl_d"], 2)
                    pe.wait_ge(S["hots_d"], 2)
                    pe.matmul(p_count, ones_h[:, :], hot_sum[:, :], start=True, stop=True).then_inc(S["cnt0_d"], 1)
                run_at(m, ema_sims)
                router_at(m, router)
                if m < HALVES - 1:
                    run_at(m, lambda _: keep_warm(WARM[m % 2]))
                else:
                    pe.wait_ge(S["mx_d"], H * HALVES)
                    pe.wait_ge(S["fam_d"], HALVES)
                    pe.wait_ge(S["onT_d"], HALVES)
                    pe.wait_ge(S["ld_w1"], 16)
                    pe.wait_ge(S["ld_w2"], 16)
                    early = early_steps(pe, tile_step)
                    early(0)
                run_at(m + 1, turn_on)
                run_at(m - 1, turn_h2)
                router_at(m, rank)
            early(1)
            router(len(GROUPS) - 2)
            rank(len(GROUPS) - 2)
            turn_h2(HALVES - 1)
            router(len(GROUPS) - 1)
            rank(len(GROUPS) - 1)
            pe.wait_ge(S["pl_d"], len(GROUPS))
            pe.wait_ge(S["hots_d"], len(GROUPS))
            pe.matmul(p_count, ones_h[:, :], hot_sum[:, :], start=True, stop=True).then_inc(S["cnt_d"], 1)
            for n in range(2, EARLY):
                early(n)
            late_steps(pe, tile_step)


_INS = ["L0_attn_x", "L0_attn_ema_out", "L0_attn_logit_decay", "L0_attn_log_tau", "L0_attn_log_blend",
        "L0_attn_logit_blend_seq", "L0_ffn_router_W", "L0_ffn_router_b", "L0_ffn_W1", "L0_ffn_b1", "L0_ffn_W2",
        "L0_ffn_b2", "L0_c", "L0_wmod"]


def kernel(**inputs):
    import numpy as np
    import concourse.bacc as bacc
    from concourse.bass_utils import run_bass_kernel_spmd as run

    nc = bacc.Bacc("TRN2", target_bir_lowering=False, num_devices=1)
    arrays, args = {}, []
    for name in _INS:
        a = np.ascontiguousarray(inputs[name])
        a = a.reshape(a.shape or (1,))
        arrays[f"in_{name}"] = a
        args.append(nc.dram_tensor(f"in_{name}", a.shape, mybir.dt.from_np(a.dtype), kind="ExternalInput").ap())
    args.append(nc.dram_tensor("out_x", (B, T, D), f32, kind="ExternalOutput").ap())
    build(nc, *args)
    return run(nc, [arrays], core_ids=[0]).results[0]["out_x"]
```
